# Optimizing a Trainium2 kernel written in Bass

```python
import numpy as np
import jax
import jax.numpy as jnp

def _softmax(x, axis=-1):
    return jax.nn.softmax(x, axis=axis)

def _gelu(x):
    return jax.nn.gelu(x, approximate=True)

def _silu(x):
    return jax.nn.silu(x)

def _sigmoid(x):
    return jax.nn.sigmoid(x)

def _layernorm(x, axis=-1, eps=1e-05):
    m = jnp.mean(x, axis=axis, keepdims=True)
    v = jnp.var(x, axis=axis, keepdims=True)
    return (x - m) / jnp.sqrt(v + eps)

def _scatter_add(tgt, idx, src, axis=0):
    return tgt.at[idx].add(src)

def _segment_sum(src, seg, n):
    return jax.ops.segment_sum(src, seg, n)
kernel_name = 'mk_seq_preln_d1_jaxref_r4_aff5db'

def setup_inputs(seed: int=0):
    np.random.seed(seed)
    _w = jnp.asarray

    def _L0_attn_setup():
        import jax, jax.numpy as jnp
        import numpy as np
        WINDOW = 16
        B, S, E, H = (2, 512, 256, 16)
        HD = E // H

        def _blocked_mask(seq_len: int) -> jnp.ndarray:
            i = jnp.arange(seq_len)[:, None]
            j = jnp.arange(seq_len)[None, :]
            return (j <= i) & (j >= i - WINDOW)
        key = jax.random.key(seed)
        k1, k2, k3, k4, k5, k6 = jax.random.split(key, 6)
        input_embeddings = jax.random.normal(k1, (B, S, E), dtype=jnp.float32)
        token_ids = jax.random.randint(k2, (B, S), 0, 8000, dtype=jnp.int64)
        in_proj_weight = jax.random.normal(k3, (3 * E, E), dtype=jnp.float32) * 0.02
        in_proj_bias = jax.random.normal(k4, (3 * E,), dtype=jnp.float32) * 0.02
        out_proj_weight = jax.random.normal(k5, (E, E), dtype=jnp.float32) * 0.02
        out_proj_bias = jax.random.normal(k6, (E,), dtype=jnp.float32) * 0.02
        return {'input_embeddings': input_embeddings, 'token_ids': token_ids, 'in_proj_weight': in_proj_weight, 'in_proj_bias': in_proj_bias, 'out_proj_weight': out_proj_weight, 'out_proj_bias': out_proj_bias}
    _L0_attn_in = _L0_attn_setup()

    def _L0_ffn_setup():
        import jax, jax.numpy as jnp
        import numpy as np
        D_MODEL = 256
        key = jax.random.key(seed)
        k_x, k_w, k_a1, k_a2 = jax.random.split(key, 4)
        x = jax.random.normal(k_x, (4, 512, D_MODEL), dtype=jnp.float32)
        weight = jax.random.normal(k_w, (D_MODEL, D_MODEL), dtype=jnp.float32) * 0.02
        aux_weight1 = jax.random.normal(k_a1, (D_MODEL, D_MODEL), dtype=jnp.float32) * 0.02
        aux_weight2 = jax.random.normal(k_a2, (D_MODEL, D_MODEL), dtype=jnp.float32) * 0.02
        bias = jnp.zeros((D_MODEL,), dtype=jnp.float32)
        return {'x': x, 'weight': weight, 'aux_weight1': aux_weight1, 'aux_weight2': aux_weight2, 'bias': bias}
    _L0_ffn_in = _L0_ffn_setup()
    _d = {'L0_attn_input_embeddings': _L0_attn_in['input_embeddings'], 'L0_attn_token_ids': _L0_attn_in['token_ids'], 'L0_attn_in_proj_weight': _L0_attn_in['in_proj_weight'], 'L0_attn_in_proj_bias': _L0_attn_in['in_proj_bias'], 'L0_attn_out_proj_weight': _L0_attn_in['out_proj_weight'], 'L0_attn_out_proj_bias': _L0_attn_in['out_proj_bias'], 'L0_ffn_weight': _L0_ffn_in['weight'], 'L0_ffn_aux_weight1': _L0_ffn_in['aux_weight1'], 'L0_ffn_aux_weight2': _L0_ffn_in['aux_weight2'], 'L0_ffn_bias': _L0_ffn_in['bias']}
    _x0 = _d['L0_attn_input_embeddings']
    _d['L0_attn_input_embeddings'] = jax.random.normal(jax.random.fold_in(jax.random.key(seed), 1), (4, 2048, 256), dtype=_x0.dtype)
    del _x0
    return _d

def reference(L0_attn_input_embeddings, L0_attn_token_ids, L0_attn_in_proj_weight, L0_attn_in_proj_bias, L0_attn_out_proj_weight, L0_attn_out_proj_bias, L0_ffn_weight, L0_ffn_aux_weight1, L0_ffn_aux_weight2, L0_ffn_bias):

    def _L0_attn_ref(input_embeddings, token_ids, in_proj_weight, in_proj_bias, out_proj_weight, out_proj_bias):
        import jax, jax.numpy as jnp
        import numpy as np
        WINDOW = 16
        B, S, E, H = (2, 512, 256, 16)
        HD = E // H

        def _blocked_mask(seq_len: int) -> jnp.ndarray:
            i = jnp.arange(seq_len)[:, None]
            j = jnp.arange(seq_len)[None, :]
            return (j <= i) & (j >= i - WINDOW)
        x = input_embeddings
        b, s, e = x.shape
        qkv = jnp.einsum('bse,fe->bsf', x, in_proj_weight) + in_proj_bias
        q, k, v = jnp.split(qkv, 3, axis=-1)
        q = q.reshape(b, s, H, HD).transpose(0, 2, 1, 3)
        k = k.reshape(b, s, H, HD).transpose(0, 2, 1, 3)
        v = v.reshape(b, s, H, HD).transpose(0, 2, 1, 3)
        scale = 1.0 / jnp.sqrt(jnp.asarray(HD, dtype=x.dtype))
        scores = jnp.einsum('bhqd,bhkd->bhqk', q * scale, k)
        blocked = _blocked_mask(s)
        scores = jnp.where(blocked[None, None, :, :], -jnp.inf, scores)
        attn = jax.nn.softmax(scores, axis=-1)
        ctx = jnp.einsum('bhqk,bhkd->bhqd', attn, v)
        ctx = ctx.transpose(0, 2, 1, 3).reshape(b, s, e)
        out = jnp.einsum('bse,fe->bsf', ctx, out_proj_weight) + out_proj_bias
        return out

    def _L0_ffn_ref(x, weight, aux_weight1, aux_weight2, bias):
        import jax, jax.numpy as jnp
        import numpy as np
        D_MODEL = 256
        h = jnp.einsum('btc,cd->btd', x, weight)
        h = jnp.einsum('btc,cd->btd', h, aux_weight1)
        h = jnp.einsum('btc,cd->btd', h, aux_weight2)
        return jnp.tanh(h + bias)
    x = L0_attn_input_embeddings
    x = x + _L0_attn_ref(_layernorm(x, axis=-1), L0_attn_token_ids, L0_attn_in_proj_weight, L0_attn_in_proj_bias, L0_attn_out_proj_weight, L0_attn_out_proj_bias)
    x = x + _L0_ffn_ref(_layernorm(x, axis=-1), L0_ffn_weight, L0_ffn_aux_weight1, L0_ffn_aux_weight2, L0_ffn_bias)
    return x

_drawn_inputs = setup_inputs


def setup_inputs(seed=0):
    import zlib

    import numpy as np

    out = dict(_drawn_inputs(seed))
    spreads = {'L0_ffn_bias': (0.0, 2.0)}
    factors = {'L0_attn_in_proj_weight': 8.0,
     'L0_attn_in_proj_bias': 8.0,
     'L0_attn_out_proj_weight': 8.0,
     'L0_attn_out_proj_bias': 12.593,
     'L0_ffn_weight': 8.0,
     'L0_ffn_aux_weight1': 8.0,
     'L0_ffn_aux_weight2': 8.0}
    for name, (base, spread) in spreads.items():
        noise = np.random.default_rng([zlib.crc32(name.encode()), seed]).standard_normal(out[name].shape)
        drawn = base * np.exp(spread * noise) if base else spread * noise
        out[name] = jnp.asarray(drawn.astype(out[name].dtype))
    for name, factor in factors.items():
        out[name] = (out[name] * factor).astype(out[name].dtype)
    return out
```

```python
from contextlib import ExitStack

import concourse.bass as bass
from concourse import mybir

F32 = mybir.dt.float32
BF16 = mybir.dt.bfloat16
I32 = mybir.dt.int32
ALU = mybir.AluOpType
ACT = mybir.ActivationFunctionType
AX = mybir.AxisListType

P = 128
BATCH, SEQ, EMB, HEADS = 4, 2048, 256, 16
HD = EMB // HEADS
WINDOW = 16
EPS = 1e-5
CHUNK = 512
CPB = SEQ // CHUNK
NCH = BATCH * CPB
TPC = CHUNK // P
HALVES = EMB // P
KBS = SEQ // P
HG = 4
PAIRS = BATCH * HALVES
PARTS = 3
Q_ROWS = (0, 0, 1, 0, 2, 1)
K_ROWS = (0, 1, 0, 2, 0, 1)
DOT = len(Q_ROWS) * HD
CONTRACT = DOT + PARTS
BAND = P + WINDOW
LEAST_SUM = 1e-26
SUM_FLOOR = 1e-30
MARGIN = 1.02
NEG = -3.0e38


def carry(eng, passed):
    eng.sem_inc(passed, 1)


def bass_preln_layer(nc, x, w_qkv_t, b_qk, b_v, w_o_t, b_o, w1_t, a1_t, a2, b_f, out):
    q_parts = nc.dram_tensor("q_parts", (PAIRS, PARTS, P, SEQ), BF16, kind="Internal").ap()
    k_parts = nc.dram_tensor("k_parts", (PAIRS, PARTS, P, SEQ), BF16, kind="Internal").ap()
    guards = nc.dram_tensor("guards", (PAIRS, PARTS, HEADS // HALVES, SEQ), BF16, kind="Internal").ap()
    v_ones = nc.dram_tensor("v_ones", (PAIRS, 2, P, KBS, HG * 2 * HD), F32, kind="Internal").ap()
    context = nc.dram_tensor("context", (PAIRS, P, SEQ), F32, kind="Internal").ap()

    with ExitStack() as ctx:
        def sb(name, shape, dt=F32):
            return ctx.enter_context(nc.sbuf_tensor(name, shape, dt))

        keep = {
            "ident": sb("ident", [P, P]),
            "w_o": sb("w_o", [P, HALVES, EMB]),
            "w_ffn": sb("w_ffn", [P, HALVES, EMB]),
            "bias_o": sb("bias_o", [P, EMB]),
            "bias_f": sb("bias_f", [P, EMB]),
            "minus_half": sb("minus_half", [P, TPC]),
            "eps": sb("eps", [P, TPC]),
        }
        project(nc, keep, x, w_qkv_t, b_qk, b_v, w_o_t, b_o, w1_t, a1_t, a2, b_f,
                q_parts, k_parts, guards, v_ones)
        attend(nc, keep, q_parts, k_parts, guards, v_ones, context)
        finish(nc, keep, x, context, out)


def project(nc, keep, x, w_qkv_t, b_qk, b_v, w_o_t, b_o, w1_t, a1_t, a2, b_f,
            q_parts, k_parts, guards, v_ones):
    with ExitStack() as ctx:
        def sb(name, shape, dt=F32):
            return ctx.enter_context(nc.sbuf_tensor(name, shape, dt))

        def bank(name, shape):
            return ctx.enter_context(nc.psum_tensor(name, shape, F32))

        def sem(name):
            return ctx.enter_context(nc.semaphore(name))

        ident = keep["ident"]
        w_qkv = sb("w_qkv", [P, HALVES, 3 * EMB])
        bias_qk = sb("bias_qk", [P, 2 * HALVES])
        bias_v = sb("bias_v", [P, EMB])
        w1t = sb("w1t", [P, HALVES, EMB])
        a1t = sb("a1t", [P, HALVES, EMB])
        a2s = sb("a2s", [P, HALVES, EMB])
        a12 = sb("a12", [P, HALVES, EMB])
        head_of = sb("head_of", [P, HALVES, HEADS], BF16)
        xin = sb("xin", [P, 2, TPC, EMB])
        stats = sb("stats", [P, TPC, 6])
        mean_var = sb("mean_var", [P, TPC, 2])
        var_eps = sb("var_eps", [P, TPC])
        rstd = sb("rstd", [P, TPC])
        xn = sb("xn", [P, TPC, EMB])
        xt = sb("xt", [P, 2, HALVES, CHUNK])
        qk_f = sb("qk_f", [P, 4, CHUNK])
        rest = sb("rest", [P, 4, CHUNK])
        squares = sb("squares", [P, 4, CHUNK], BF16)
        parts = sb("parts", [P, 2, 4, PARTS, CHUNK], BF16)
        vaug = sb("vaug", [P, 2, HALVES * 2, TPC, HG, 2 * HD])
        q_sq = sb("q_sq", [HEADS, SEQ])
        k_sq = sb("k_sq", [HEADS, CPB])
        k_max = sb("k_max", [HEADS, 1])
        bound = sb("bound", [HEADS, SEQ])
        guard = sb("guard", [HEADS, PARTS, SEQ], BF16)

        ps_turn = [bank("ps_turn1", [P, CHUNK]), bank("ps_turn0", [P, CHUNK])]
        ps_norm = ps_turn[1]
        ps_qk = bank("ps_qk", [P, 4, CHUNK])
        ps_v = bank("ps_v", [P, TPC, EMB])

        passed = sem("passed")
        weights_in = sem("weights_in")
        consts = sem("consts")
        a12_ready = sem("a12_ready")
        a12_copied = sem("a12_copied")
        x_in = [sem("x_in0"), sem("x_in1")]
        stats_step = sem("stats_step")
        stats_done = sem("stats_done")
        eps_added = sem("eps_added")
        rstd_done = sem("rstd_done")
        xn_done = sem("xn_done")
        turned = sem("turned")
        turn_copied = sem("turn_copied")
        qk_ready = sem("qk_ready")
        qk_copied = sem("qk_copied")
        squared = sem("squared")
        q_bias_scaled = sem("q_bias_scaled")
        rest_done = sem("rest_done")
        mid_done = sem("mid_done")
        low_done = sem("low_done")
        v_ready = sem("v_ready")
        v_copied = sem("v_copied")
        norms_ready = sem("norms_ready")
        norms_copied = sem("norms_copied")
        k_max_done = sem("k_max_done")
        bound_done = sem("bound_done")
        guard_done = sem("guard_done")
        parts_out = [sem("parts_out0"), sem("parts_out1")]
        v_out = [sem("v_out0"), sem("v_out1")]
        guard_out = sem("guard_out")

        WEIGHTS = 9
        x_tiles = x.rearrange("(c t p) e -> c p t e", t=TPC, p=P)
        block = ctx.enter_context(nc.Block())

        def over_chunks(eng, step):
            with eng.Fori(0, BATCH - 1) as b:
                for cc in range(CPB):
                    step(b * CPB + cc, b, cc, True)
            for cc in range(CPB):
                step((BATCH - 1) * CPB + cc, BATCH - 1, cc, cc < CPB - 1)

        def uses(b, cc):
            return b * (CPB // 2) + cc // 2

        @block.sync
        def _(sp):
            sp.dma_start(xin[:, 0], x_tiles[0]).then_inc(x_in[0], 16)
            sp.dma_start(xin[:, 1], x_tiles[1]).then_inc(x_in[1], 16)
            for dst, src in ((w_qkv, w_qkv_t), (keep["w_o"], w_o_t), (w1t, w1_t), (a1t, a1_t), (a2s, a2)):
                sp.dma_start(dst[:], src.rearrange("(h p) n -> p h n", p=P)).then_inc(weights_in, 16)
            sp.dma_start(bias_qk[:], b_qk).then_inc(weights_in, 16)
            for dst, src in ((bias_v, b_v), (keep["bias_o"], b_o), (keep["bias_f"], b_f)):
                sp.dma_start(dst[:], src.partition_broadcast(P)).then_inc(weights_in, 16)

            def store(c, b, cc, more):
                par = cc % 2
                last_two = isinstance(b, int) and cc >= CPB - 2
                if not last_two:
                    sp.wait_ge(xn_done, c + 1)
                    carry(sp, passed)
                    nxt = c + 2
                    src = x_tiles[nxt] if isinstance(nxt, int) else x_tiles[bass.ds(nxt, 1)].rearrange(
                        "o p t e -> (o p) t e")
                    sp.dma_start(xin[:, par], src).then_inc(x_in[par], 16)
                for j in range(4):
                    sp.wait_ge(low_done, c * 4 + j + 1 + 4)
                    carry(sp, passed)
                    dst = (q_parts, k_parts)[j // 2]
                    n = b * HALVES + j % 2
                    view = dst[bass.ds(n, 1), :, :, cc * CHUNK:(cc + 1) * CHUNK].rearrange("o a p t -> p (o a) t")
                    sp.dma_start(view, parts[:, par, j]).then_inc(parts_out[par], 16)
                sp.wait_ge(v_copied, c * TPC + TPC + TPC)
                carry(sp, passed)
                view = v_ones[bass.ds(b * HALVES, HALVES), :, :, cc * TPC:(cc + 1) * TPC].rearrange(
                    "f g p k n -> p (f g) (k n)")
                sp.dma_start(view, vaug[:, par].rearrange("p g k h n -> p g (k h n)")).then_inc(v_out[par], 16)
                if cc == CPB - 1:
                    sp.wait_ge(guard_done, b + 1)
                    carry(sp, passed)
                    for half in range(HALVES):
                        view = guards[bass.ds(b * HALVES + half, 1)].rearrange("o a h t -> h (o a) t")
                        sp.dma_start(view, guard[half * 8:half * 8 + 8]).then_inc(guard_out, 16)

            over_chunks(sp, store)
            for par in range(2):
                sp.wait_ge(parts_out[par], NCH // 2 * 64)
                sp.wait_ge(v_out[par], NCH // 2 * 16)
            sp.wait_ge(guard_out, BATCH * 32)

        @block.gpsimd
        def _(pool):
            pool.memset(ident[:], 0.0).then_inc(consts, 1)
            pool.memset(head_of[:], 1.0).then_inc(consts, 1)
            pool.memset(keep["minus_half"][:], -0.5).then_inc(consts, 1)
            pool.memset(keep["eps"][:], EPS).then_inc(consts, 1)
            pool.memset(guard[:], 0.0).then_inc(consts, 1)
            pool.memset(vaug[:], 1.0).then_inc(consts, 1)
            pool.wait_ge(consts, 6)
            pool.affine_select(out=ident[:], in_=ident[:], compare_op=ALU.not_equal, fill=1.0, base=0,
                               pattern=[[-1, P]], channel_multiplier=1).then_inc(consts, 1)
            pool.affine_select(out=head_of[:], in_=head_of[:], compare_op=ALU.is_ge, fill=0.0, base=0,
                               pattern=[[P, HALVES], [-HD, HEADS]], channel_multiplier=1).then_inc(consts, 1)
            pool.wait_ge(consts, 8)
            pool.affine_select(out=head_of[:], in_=head_of[:], compare_op=ALU.is_ge, fill=0.0, base=HD - 1,
                               pattern=[[-P, HALVES], [HD, HEADS]], channel_multiplier=-1).then_inc(consts, 1)

            def rsqrt(c):
                pool.wait_ge(stats_done, c + 1)
                pool.tensor_tensor(var_eps[:], mean_var[:, :, 1], keep["eps"][:], ALU.add).then_inc(eps_added, 1)
                pool.wait_ge(eps_added, c + 1)
                pool.tensor_tensor(rstd[:], var_eps[:], keep["minus_half"][:], ALU.pow).then_inc(rstd_done, 1)

            with pool.Fori(0, NCH) as c:
                rsqrt(c)

        @block.vector
        def _(dve):
            dve.sem_inc(low_done, 4)
            dve.sem_inc(v_copied, TPC)

            def normalise_a(c, b, cc):
                par = cc % 2
                dve.wait_ge(x_in[par], uses(b, cc) * 16 + 16)
                for t in range(TPC):
                    dve.bn_stats(stats[:, t], xin[:, par, t]).then_inc(stats_step, 1)
                dve.wait_ge(stats_step, c * TPC + TPC)
                carry(dve, passed)
                for t in range(TPC):
                    last = dve.bn_aggr(mean_var[:, t], stats[:, t])
                last.then_inc(stats_done, 1)

            def normalise_b(c, b, cc):
                par = cc % 2
                dve.wait_ge(stats_done, c + 1)
                dve.wait_ge(rstd_done, c + 1)
                dve.wait_ge(turned, c * 2)
                for t in range(TPC):
                    last = dve.tensor_scalar(xn[:, t], xin[:, par, t], mean_var[:, t, 0:1], rstd[:, t:t + 1],
                                             ALU.subtract, ALU.mult)
                last.then_inc(xn_done, 1)

            def split(c, b, cc, j):
                par = cc % 2
                dve.wait_ge(qk_copied, c * 4 + j + 1)
                dve.tensor_tensor(rest[:, j], qk_f[:, j], parts[:, par, j, 0], ALU.subtract).then_inc(rest_done, 1)
                dve.wait_ge(rest_done, c * 4 + j + 1)
                dve.tensor_copy(parts[:, par, j, 1], rest[:, j]).then_inc(mid_done, 1)
                dve.wait_ge(mid_done, c * 4 + j + 1)
                dve.tensor_tensor(parts[:, par, j, 2], rest[:, j], parts[:, par, j, 1],
                                  ALU.subtract).then_inc(low_done, 1)

            def step(c, b, cc, more):
                par = cc % 2
                dve.wait_ge(parts_out[par], uses(b, cc) * 64)
                dve.wait_ge(v_out[par], uses(b, cc) * 16)
                nb, ncc = (b, cc + 1) if cc < CPB - 1 else (b + 1, 0)
                if more:
                    normalise_a(c + 1, nb, ncc)
                split(c, b, cc, 0)
                if more:
                    normalise_b(c + 1, nb, ncc)
                for j in range(1, 4):
                    split(c, b, cc, j)
                for t in range(TPC):
                    dve.wait_ge(v_ready, c * TPC + 2 * (t // 2) + 2)
                    dve.tensor_tensor(
                        vaug[:, par, :, t, :, 0:HD],
                        ps_v[:, t].rearrange("p (g h d) -> p g h d", g=HALVES * 2, h=HG),
                        bias_v[:].rearrange("p (g h d) -> p g h d", g=HALVES * 2, h=HG),
                        ALU.add).then_inc(v_copied, 1)
                dve.wait_ge(norms_ready, c + 1)
                if cc == 0:
                    dve.wait_ge(bound_done, b)
                dve.tensor_copy(q_sq[:, cc * CHUNK:(cc + 1) * CHUNK], ps_norm[0:HEADS]).then_inc(norms_copied, 1)
                dve.tensor_reduce(k_sq[:, cc:cc + 1], ps_norm[32:32 + HEADS], AX.X, ALU.max).then_inc(norms_copied, 1)
                if cc == CPB - 1:
                    dve.wait_ge(norms_copied, c * 2 + 2)
                    dve.tensor_reduce(k_max[:], k_sq[:], AX.X, ALU.max).then_inc(k_max_done, 1)
                    dve.wait_ge(bound_done, b + 1)
                    dve.wait_ge(guard_out, b * 32)
                    dve.tensor_scalar(guard[:, 0], bound[:], -MARGIN, None, ALU.mult).then_inc(guard_done, 1)

            normalise_a(0, 0, 0)
            dve.wait_ge(consts, 9)
            for half in range(HALVES):
                dve.wait_ge(a12_ready, HALVES)
                dve.tensor_copy(a12[:, half], ps_v[:, half]).then_inc(a12_copied, 1)
            for half in range(HALVES):
                dve.wait_ge(a12_ready, 2 * HALVES)
                dve.tensor_copy(keep["w_ffn"][:, half], ps_v[:, 2 + half]).then_inc(a12_copied, 1)
            normalise_b(0, 0, 0)
            over_chunks(dve, step)

        @block.scalar
        def _(act):
            act.sem_inc(squared, 4)
            act.wait_ge(weights_in, WEIGHTS * 16)
            act.activation(bias_qk[:, 0:HALVES], bias_qk[:, 0:HALVES], ACT.Copy, scale=HD ** -0.5).then_inc(q_bias_scaled, 1)
            act.wait_ge(q_bias_scaled, 1)

            def copy_turned(c, cc):
                for half in range(HALVES):
                    act.wait_ge(turned, c * 2 + half + 1)
                    act.activation(xt[:, cc % 2, half], ps_turn[half][:], ACT.Identity).then_inc(turn_copied, 1)

            def step(c, b, cc, more):
                par = cc % 2
                act.wait_ge(parts_out[par], uses(b, cc) * 64)
                for j in range(4):
                    scale = HD ** -0.5 if j < HALVES else 1.0
                    act.wait_ge(qk_ready, c * 4 + j + 1)
                    act.wait_ge(low_done, c * 4 + j + 1)
                    act.activation(qk_f[:, j], ps_qk[:, j], ACT.Identity, bias=bias_qk[:, j:j + 1], scale=scale)
                    act.activation(parts[:, par, j, 0], ps_qk[:, j], ACT.Identity, bias=bias_qk[:, j:j + 1],
                                   scale=scale).then_inc(qk_copied, 1)
                    act.wait_ge(norms_ready, c)
                    act.activation(squares[:, j], ps_qk[:, j], ACT.Square, bias=bias_qk[:, j:j + 1],
                                   scale=scale).then_inc(squared, 1)
                if more:
                    copy_turned(c + 1, cc + 1)
                if cc == CPB - 1:
                    act.wait_ge(k_max_done, b + 1)
                    act.wait_ge(guard_done, b)
                    act.activation(bound[:], q_sq[:], ACT.Sqrt, scale=k_max[:]).then_inc(bound_done, 1)

            copy_turned(0, 0)
            over_chunks(act, step)

        @block.tensor
        def _(pe):
            def turn(c, half):
                carry(pe, passed)
                for t in range(TPC):
                    last = pe.transpose(ps_turn[half][:, t * P:(t + 1) * P], xn[:, t, half * P:(half + 1) * P],
                                        ident[:])
                last.then_inc(turned, 1)

            pe.wait_ge(weights_in, WEIGHTS * 16)
            for stage, (left, right) in enumerate(((a1t, a2s), (w1t, a12))):
                if stage:
                    pe.wait_ge(a12_copied, HALVES)
                for half in range(HALVES):
                    for k in range(HALVES):
                        last = pe.matmul(ps_v[:, 2 * stage + half], left[:, k, half * P:(half + 1) * P], right[:, k],
                                         start=(k == 0), stop=(k == HALVES - 1))
                    last.then_inc(a12_ready, 1)
            pe.wait_ge(consts, 9)
            pe.wait_ge(xn_done, 1)
            turn(0, 0)
            turn(0, 1)
            pe.wait_ge(a12_copied, 2 * HALVES)

            def step(c, b, cc, more):
                par = cc % 2
                pe.wait_ge(turn_copied, c * 2 + 2)
                for j in range(4):
                    pe.wait_ge(squared, c * 4 + j + 1)
                    for k in range(HALVES):
                        last = pe.matmul(ps_qk[:, j], w_qkv[:, k, j * P:(j + 1) * P], xt[:, par, k],
                                         start=(k == 0), stop=(k == HALVES - 1))
                    last.then_inc(qk_ready, 1)
                if more:
                    pe.wait_ge(xn_done, c + 2)
                    turn(c + 1, 0)
                pe.wait_ge(norms_copied, c * 2)
                if more:
                    turn(c + 1, 1)
                for t in range(TPC):
                    pe.wait_ge(v_copied, c * TPC + 2 * (t // 2) + 2)
                    for k in range(HALVES):
                        last = pe.matmul(ps_v[:, t], xt[:, par, k, t * P:(t + 1) * P], w_qkv[:, k, 2 * EMB:],
                                         start=(k == 0), stop=(k == HALVES - 1))
                    last.then_inc(v_ready, 1)
                pe.wait_ge(squared, c * 4 + 4 + 4)
                if more:
                    pe.wait_ge(turn_copied, c * 2 + 4)
                for j in range(4):
                    at = 32 * (j // 2)
                    last = pe.matmul(ps_norm[at:at + HEADS], head_of[:, j % 2], squares[:, j],
                                     start=(j % 2 == 0), stop=(j % 2 == 1))
                last.then_inc(norms_ready, 1)

            over_chunks(pe, step)


def attend(nc, keep, q_parts, k_parts, guards, v_ones, context):
    with ExitStack() as ctx:
        def sb(name, shape, dt=F32):
            return ctx.enter_context(nc.sbuf_tensor(name, shape, dt))

        def sem(name):
            return ctx.enter_context(nc.semaphore(name))

        RING = 32
        SBANKS = 6
        qs = sb("qs", [CONTRACT, 2, HG, SEQ], BF16)
        ks = sb("ks", [CONTRACT, 2, HG, SEQ], BF16)
        vs = sb("vs", [P, 2, KBS, HG, 2 * HD])
        probs = sb("probs", [P, RING, CHUNK])
        allowed = sb("allowed", [P, BAND])
        blocked = sb("blocked", [P, BAND])
        blocked_bf = sb("blocked_bf", [P, BAND], BF16)
        ident_bf = sb("ident_bf", [P, P], BF16)
        sums = sb("sums", [P, CHUNK])
        inverse = sb("inverse", [P, CHUNK])
        ctx_t = sb("ctx_t", [P, 2, CHUNK])
        sums_fine = sb("sums_fine", [P, CHUNK])
        fine = sb("fine", [P, 1])
        bad = sb("bad", [P, 1])
        any_bad = sb("any_bad", [P, 1])
        flag = sb("flag", [1, 1], I32)
        row_max = sb("row_max", [P, HG * KBS])
        guard_f = sb("guard_f", [HG * KBS, P])
        guard_rest = sb("guard_rest", [HG * KBS, P])
        guard_parts = sb("guard_parts", [HG * KBS, PARTS, P], BF16)
        scores = ctx.enter_context(nc.psum_tensor("scores", [P, SBANKS, CHUNK], F32))
        outs = ctx.enter_context(nc.psum_tensor("outs", [P, 2, CHUNK], F32))

        passed = sem("a_passed")
        consts = sem("a_consts")
        fine_ready = sem("fine_ready")
        all_bad = sem("all_bad")
        flag_ready = sem("flag_ready")
        tile_ring = scores[:].rearrange("p b q -> p (b q)")
        prob_ring = probs[:].rearrange("p b q -> p (b q)")

        TILES = 2 * CPB * KBS * HG
        EXPS = TILES // 2
        UNITS = TILES // HG
        STEPS = 2 * CPB
        SPARE = RING // HG

        def masked_units():
            found = {}
            for s in range(STEPS):
                qc = s % CPB
                for kb in range(KBS):
                    at = kb * P - qc * CHUNK
                    lo, hi = max(at, 0), min(at + BAND, CHUNK)
                    if lo < hi:
                        found[s * KBS + kb] = (lo, hi - lo, lo - at)
            return found

        MASKED = masked_units()
        MASKS = 2 * len(MASKED)

        class Run:
            def __init__(self, tag):
                self.loaded = [sem(f"{tag}_loaded0"), sem(f"{tag}_loaded1")]
                self.scored = sem(f"{tag}_scored")
                self.exped = sem(f"{tag}_exped")
                self.masked = sem(f"{tag}_masked")
                self.summed = sem(f"{tag}_summed")
                self.out_free = sem(f"{tag}_out_free")
                self.shuffled = sem(f"{tag}_shuffled")
                self.inverted = sem(f"{tag}_inverted")
                self.checked = sem(f"{tag}_checked")
                self.stored = [sem(f"{tag}_stored0"), sem(f"{tag}_stored1")]

        EVACUATE_AT = {0: 5, 1: 9, 2: 3, 3: 4}

        def over_pairs(eng, body):
            with eng.Fori(0, PAIRS - 1) as n:
                body(n, True)
            body(PAIRS - 1, False)

        def bank_pair(e):
            return 1 if e == EXPS - 1 else e % (SBANKS // 2)

        def bank_user(e):
            before = max(x for x in range(-EXPS, e) if bank_pair(x % EXPS) == bank_pair(e))
            return before + 1

        first, again = Run("first"), Run("again")
        LOADS = 2 * len(Q_ROWS) + 2

        def load(sp, n, par, loaded, values=True):
            def src(parts_dram, part):
                return parts_dram[bass.ds(n, 1), part, par * 64:par * 64 + 64].rearrange(
                    "o (h d) t -> d (o h) t", h=HG)
            for r in range(len(Q_ROWS)):
                rows = slice(r * HD, (r + 1) * HD)
                sp.dma_start(qs[rows, par], src(q_parts, Q_ROWS[r])).then_inc(loaded, 16)
                sp.dma_start(ks[rows, par], src(k_parts, K_ROWS[r])).then_inc(loaded, 16)
            if values:
                sp.dma_start(qs[DOT:CONTRACT, par],
                             guards[bass.ds(n, 1), :, par * HG:(par + 1) * HG].rearrange(
                                 "o a h t -> (o a) h t")).then_inc(loaded, 16)
                sp.dma_start(vs[:, par].rearrange("p k h n -> p (k h n)"),
                             v_ones[bass.ds(n, 1), par].rearrange("o p k n -> (o p) (k n)")).then_inc(loaded, 16)

        def run_sync(sp, r):
            for par in range(2):
                load(sp, 0, par, r.loaded[par])

            def body(n, more):
                for par in range(2):
                    for qc in range(CPB):
                        s = par * CPB + qc
                        sp.wait_ge(r.checked, n * STEPS + s + 1)
                        carry(sp, passed)
                        for g in range(HG):
                            at = par * 64 + g * HD
                            sp.dma_start(
                                context[bass.ds(n, 1), at:at + HD, qc * CHUNK:(qc + 1) * CHUNK].rearrange(
                                    "o d t -> (o d) t"),
                                ctx_t[32 * g:32 * g + HD, s % 2]).then_inc(r.stored[s % 2], 16)
                    if more:
                        sp.wait_ge(r.summed, n * UNITS + (par + 1) * UNITS // 2 + SPARE)
                        carry(sp, passed)
                        load(sp, n + 1, par, r.loaded[par])

            over_pairs(sp, body)
            for par in range(2):
                sp.wait_ge(r.stored[par], PAIRS * CPB * 64)

        def run_tensor(pe, r, block_first):
            def score(n, u):
                s, kb = divmod(u, KBS)
                par, qc = divmod(s, CPB)
                if kb == 0 and qc == 0:
                    pe.wait_ge(r.loaded[par], n * (LOADS * 16) + LOADS * 16)
                for h in range(HG):
                    e, side = divmod(u * HG + h, 2)
                    bank = 2 * bank_pair(e) + side
                    done = bank_user(e)
                    if side == 0 and not (done <= 0 and isinstance(n, int) and n == 0):
                        pe.wait_ge(r.exped, n * EXPS + done)
                    add = block_first and u in MASKED
                    last = pe.matmul(scores[:, bank], ks[:, par, h, kb * P:(kb + 1) * P],
                                     qs[:, par, h, qc * CHUNK:(qc + 1) * CHUNK], start=True, stop=not add)
                    if add:
                        lo, cols, at = MASKED[u]
                        last = pe.matmul(scores[:, bank, lo:lo + cols], ident_bf[:],
                                         blocked_bf[:, at:at + cols], start=False, stop=True)
                    if side == 1:
                        last.then_inc(r.scored, 1)

            def weigh(n, u):
                s, kb = divmod(u, KBS)
                par = s // CPB
                if kb == 0:
                    pe.wait_ge(r.out_free, n * STEPS + s + 1)
                pe.wait_ge(r.exped, n * EXPS + 2 * u + 2)
                if u in MASKED:
                    pe.wait_ge(r.masked, n * MASKS + 2 * (1 + sorted(MASKED).index(u)))
                for h in range(HG):
                    last = pe.matmul(outs[32 * h:32 * h + 32, s % 2], vs[:, par, kb, h],
                                     probs[:, (u * HG + h) % RING], start=(kb == 0), stop=(kb == KBS - 1))
                last.then_inc(r.summed, 1)

            def body(n, more):
                for u in range(UNITS):
                    if u + 2 < UNITS:
                        score(n, u + 2)
                    elif more:
                        score(n + 1, u + 2 - UNITS)
                    weigh(n, u)

            score(0, 0)
            score(0, 1)
            over_pairs(pe, body)

        def run_scalar(act, r):
            with act.Fori(0, PAIRS) as n:
                for e in range(EXPS):
                    act.wait_ge(r.scored, n * EXPS + e + 1)
                    act.wait_ge(r.summed, n * UNITS + (2 * e) // HG + 1)
                    a, b = 2 * bank_pair(e) * CHUNK, 2 * e % RING * CHUNK
                    act.activation(prob_ring[:, b:b + 2 * CHUNK], tile_ring[:, a:a + 2 * CHUNK],
                                   ACT.Exp).then_inc(r.exped, 1)

        def run_vector(dve, r):
            dve.sem_inc(r.summed, SPARE)
            dve.memset(sums_fine[:], 1.0).then_inc(r.out_free, 2)
            dve.wait_ge(r.out_free, 2)

            def evacuate(n, s):
                dve.wait_ge(r.summed, n * UNITS + (s + 1) * KBS + SPARE)
                dve.wait_ge(r.checked, n * STEPS + s)
                carry(dve, passed)
                dve.stream_shuffle(sums[:], outs[:, s % 2], mask=[HD] * 32).then_inc(r.shuffled, 1)
                dve.wait_ge(r.shuffled, n * STEPS + s + 1)
                dve.tensor_scalar(inverse[:], sums[:], SUM_FLOOR, None, ALU.max).then_inc(r.inverted, 1)
                dve.wait_ge(r.inverted, n * (2 * STEPS) + 2 * s + 1)
                dve.reciprocal(inverse[:], inverse[:]).then_inc(r.inverted, 1)
                dve.wait_ge(r.inverted, n * (2 * STEPS) + 2 * s + 2)
                dve.wait_ge(r.stored[s % 2], (n * (STEPS // 2) + s // 2) * 64)
                dve.tensor_tensor(ctx_t[:, s % 2], outs[:, s % 2], inverse[:], ALU.mult).then_inc(r.out_free, 1)
                dve.scalar_tensor_tensor(out=sums_fine[:], in0=sums[:], scalar=LEAST_SUM, in1=sums_fine[:],
                                         op0=ALU.is_ge, op1=ALU.mult).then_inc(r.checked, 1)

            def mask(n, u):
                lo, cols, at = MASKED[u]
                for e in (2 * u, 2 * u + 1):
                    dve.wait_ge(r.exped, n * EXPS + e + 1)
                    tiles = probs[:, 2 * e % RING:2 * e % RING + 2, lo:lo + cols]
                    keep_row = allowed[:, at:at + cols].unsqueeze(1).to_broadcast([P, 2, cols])
                    dve.tensor_tensor(tiles, tiles, keep_row, ALU.mult).then_inc(r.masked, 1)

            EARLY = EVACUATE_AT[0]

            def body(n, more):
                for u in range(EARLY, UNITS):
                    if u in MASKED:
                        mask(n, u)
                    s, kb = divmod(u, KBS)
                    if s and kb == EVACUATE_AT[s % CPB]:
                        evacuate(n, s - 1)
                for u in range(EARLY):
                    if more and u in MASKED:
                        mask(n + 1, u)
                evacuate(n, STEPS - 1)

            for u in range(EARLY):
                if u in MASKED:
                    mask(0, u)
            over_pairs(dve, body)

        g_loaded = sem("g_loaded")
        g_scored = sem("g_scored")
        g_blocked = sem("g_blocked")
        g_maxed = sem("g_maxed")
        g_turned = sem("g_turned")
        g_high = sem("g_high")
        g_step = sem("g_step")
        g_ready = sem("g_ready")
        g_stored = sem("g_stored")
        g_through = sem("g_through")
        ROWS = HG * KBS
        G_LOADS = 2 * len(Q_ROWS) * 16

        def groups(eng, body):
            with eng.Fori(0, PAIRS) as n:
                for par in range(2):
                    body(n, par, n * 2 + par)

        def maxima_sync(sp):
            def body(n, par, g):
                sp.wait_ge(g_maxed, g * ROWS)
                carry(sp, passed)
                load(sp, n, par, g_loaded, values=False)
                sp.wait_ge(g_ready, g + 1)
                carry(sp, passed)
                dst = guards[bass.ds(n, 1), :, par * HG:(par + 1) * HG].rearrange(
                    "o a h (k q) -> (o h k) a q", q=P)
                sp.dma_start(dst, guard_parts[:]).then_inc(g_stored, 16)
                sp.wait_ge(g_stored, g * 16 + 16)
                carry(sp, passed)
            groups(sp, body)

        def maxima_tensor(pe):
            def body(n, par, g):
                pe.wait_ge(g_loaded, g * G_LOADS + G_LOADS)
                for row in range(ROWS):
                    h, qb = divmod(row, KBS)
                    pe.wait_ge(g_maxed, g * ROWS + row)
                    for c in range(CPB):
                        last = pe.matmul(scores[:, c], qs[0:DOT, par, h, qb * P:(qb + 1) * P],
                                         ks[0:DOT, par, h, c * CHUNK:(c + 1) * CHUNK], start=True, stop=True)
                    last.then_inc(g_scored, 1)
                pe.wait_ge(g_maxed, g * ROWS + ROWS)
                carry(pe, passed)
                pe.transpose(outs[0:ROWS, 0, 0:P], row_max[:], keep["ident"][:]).then_inc(g_turned, 1)
            groups(pe, body)

        def maxima_vector(dve):
            def body(n, par, g):
                for row in range(ROWS):
                    qb = row % KBS
                    lo = max(qb * P - WINDOW, 0)
                    at = lo - (qb * P - WINDOW)
                    dve.wait_ge(g_scored, g * ROWS + row + 1)
                    band = tile_ring[:, lo:qb * P + P]
                    dve.tensor_tensor(band, band, blocked[:, at:BAND], ALU.add).then_inc(g_blocked, 1)
                    dve.wait_ge(g_blocked, g * ROWS + row + 1)
                    if row == 0:
                        dve.wait_ge(g_turned, g)
                    dve.tensor_reduce(row_max[:, row:row + 1], tile_ring[:, 0:SEQ], AX.X,
                                      ALU.max).then_inc(g_maxed, 1)
                dve.wait_ge(g_turned, g + 1)
                dve.wait_ge(g_stored, g * 16)
                dve.tensor_scalar(guard_f[:], outs[0:ROWS, 0, 0:P], -1.0, None, ALU.mult).then_inc(g_step, 1)
                dve.wait_ge(g_step, g * 4 + 1)
                dve.tensor_copy(guard_parts[:, 0], guard_f[:]).then_inc(g_step, 1)
                dve.wait_ge(g_step, g * 4 + 2)
                dve.tensor_tensor(guard_rest[:], guard_f[:], guard_parts[:, 0], ALU.subtract).then_inc(g_step, 1)
                dve.wait_ge(g_step, g * 4 + 3)
                dve.tensor_copy(guard_parts[:, 1], guard_rest[:]).then_inc(g_step, 1)
                dve.wait_ge(g_step, g * 4 + 4)
                dve.tensor_tensor(guard_parts[:, 2], guard_rest[:], guard_parts[:, 1],
                                  ALU.subtract).then_inc(g_ready, 1)
            groups(dve, body)

        block = ctx.enter_context(nc.Block())

        def if_bad(eng, body):
            eng.wait_ge(flag_ready, 1)
            found = eng.value_load(flag[0:1, 0:1], min_val=0, max_val=1)
            with eng.If(found > 0):
                body()

        @block.sync
        def _(sp):
            sp.wait_ge(consts, 7)
            run_sync(sp, first)

            def general():
                maxima_sync(sp)
                run_sync(sp, again)
            if_bad(sp, general)

        @block.gpsimd
        def _(pool):
            pool.memset(allowed[:], 0.0).then_inc(consts, 1)
            pool.wait_ge(consts, 2)
            pool.affine_select(out=allowed[:], in_=allowed[:], compare_op=ALU.is_ge, fill=1.0, base=0,
                               pattern=[[1, BAND]], channel_multiplier=-1).then_inc(consts, 1)
            pool.wait_ge(consts, 3)
            pool.affine_select(out=allowed[:], in_=allowed[:], compare_op=ALU.is_ge, fill=1.0, base=WINDOW,
                               pattern=[[-1, BAND]], channel_multiplier=1).then_inc(consts, 1)
            pool.wait_ge(consts, 4)
            pool.tensor_scalar(blocked[:], allowed[:], 1.0, -NEG, ALU.subtract, ALU.mult).then_inc(consts, 1)
            pool.tensor_copy(ident_bf[:], keep["ident"][:]).then_inc(consts, 1)
            pool.wait_ge(consts, 6)
            pool.tensor_copy(blocked_bf[:], blocked[:]).then_inc(consts, 1)
            pool.wait_ge(fine_ready, 2)
            pool.partition_all_reduce(any_bad[:], bad[:], P, bass.bass_isa.ReduceOp.max).then_inc(all_bad, 1)

        @block.tensor
        def _(pe):
            pe.wait_ge(consts, 7)
            run_tensor(pe, first, False)

            def general():
                maxima_tensor(pe)
                pe.wait_ge(g_ready, 2 * PAIRS)
                run_tensor(pe, again, True)
            if_bad(pe, general)

        @block.scalar
        def _(act):
            run_scalar(act, first)
            if_bad(act, lambda: run_scalar(act, again))

        @block.vector
        def _(dve):
            dve.memset(ks[DOT:CONTRACT], 1.0).then_inc(consts, 1)
            dve.wait_ge(consts, 7)
            run_vector(dve, first)
            dve.wait_ge(first.checked, PAIRS * STEPS)
            dve.tensor_reduce(fine[:], sums_fine[:], AX.X, ALU.min).then_inc(fine_ready, 1)
            dve.wait_ge(fine_ready, 1)
            dve.tensor_scalar(bad[:], fine[:], -1.0, 1.0, ALU.mult, ALU.add).then_inc(fine_ready, 1)
            dve.wait_ge(all_bad, 1)
            dve.tensor_copy(flag[:], any_bad[0:1]).then_inc(flag_ready, 1)

            def general():
                maxima_vector(dve)
                run_vector(dve, again)
            if_bad(dve, general)


def finish(nc, keep, x, context, out):
    with ExitStack() as ctx:
        def sb(name, shape, dt=F32):
            return ctx.enter_context(nc.sbuf_tensor(name, shape, dt))

        def bank(name, shape):
            return ctx.enter_context(nc.psum_tensor(name, shape, F32))

        def sem(name):
            return ctx.enter_context(nc.semaphore(name))

        ident = keep["ident"]
        ctx_in = sb("ctx_in", [P, 2, HALVES, CHUNK])
        xin = sb("f_xin", [P, 2, TPC, EMB])
        xb = sb("xb", [P, 2, TPC, EMB])
        x2 = sb("x2", [P, 2, TPC, EMB])
        stats = sb("f_stats", [P, TPC, 6])
        mean_var = sb("f_mean_var", [P, TPC, 2])
        var_eps = sb("f_var_eps", [P, TPC])
        rstd = sb("f_rstd", [P, TPC])
        xn = sb("f_xn", [P, TPC, EMB])
        xt = sb("f_xt", [P, HALVES, CHUNK])
        pre = sb("pre", [P, TPC, EMB])
        squashed = sb("squashed", [P, TPC, EMB])
        result = sb("result", [P, 2, TPC, EMB])
        ps_y = bank("ps_y", [P, TPC, EMB])
        ps_turn = bank("ps_turn", [P, HALVES, CHUNK])
        ps_f = bank("ps_f", [P, TPC, EMB])

        passed = sem("f_passed")
        data_in = [sem("data_in0"), sem("data_in1")]
        biased = sem("biased")
        y_ready = sem("y_ready")
        x2_done = sem("x2_done")
        stats_step = sem("f_stats_step")
        stats_done = sem("f_stats_done")
        eps_added = sem("f_eps_added")
        rstd_done = sem("f_rstd_done")
        xn_done = sem("f_xn_done")
        turned = sem("f_turned")
        turn_copied = sem("f_turn_copied")
        f_ready = sem("f_ready")
        pre_done = sem("pre_done")
        squash_done = sem("squash_done")
        result_done = sem("result_done")
        stored = [sem("f_stored0"), sem("f_stored1")]

        x_tiles = x.rearrange("(c t p) e -> c p t e", t=TPC, p=P)
        out_tiles = out.rearrange("(c t p) e -> c p t e", t=TPC, p=P)
        ctx_view = context.rearrange("(b f) p t -> b p f t", f=HALVES)
        block = ctx.enter_context(nc.Block())

        def over_chunks(eng, step):
            with eng.Fori(0, BATCH - 1) as b:
                for cc in range(CPB):
                    step(b * CPB + cc, b, cc, True)
            for cc in range(CPB):
                step((BATCH - 1) * CPB + cc, BATCH - 1, cc, cc < CPB - 1)

        def uses(b, cc):
            return b * (CPB // 2) + cc // 2

        def after(b, cc, k):
            return (b + (cc + k) // CPB, (cc + k) % CPB)

        @block.sync
        def _(sp):
            def load(c, b, cc):
                par = cc % 2
                sp.dma_start(ctx_in[:, par], ctx_view[bass.ds(b, 1), :, :, cc * CHUNK:(cc + 1) * CHUNK].rearrange(
                    "o p f t -> (o p) f t")).then_inc(data_in[par], 16)
                sp.dma_start(xin[:, par], x_tiles[bass.ds(c, 1)].rearrange("o p t e -> (o p) t e")
                             ).then_inc(data_in[par], 16)

            def step(c, b, cc, more):
                last_two = isinstance(b, int) and cc >= CPB - 2
                if not last_two:
                    sp.wait_ge(y_ready, c * TPC + TPC)
                    carry(sp, passed)
                    sp.wait_ge(biased, c + 1)
                    carry(sp, passed)
                    load(c + 2, *after(b, cc, 2))
                sp.wait_ge(result_done, c + 1)
                carry(sp, passed)
                sp.dma_start(out_tiles[bass.ds(c, 1)].rearrange("o p t e -> (o p) t e"),
                             result[:, cc % 2]).then_inc(stored[cc % 2], 16)

            load(0, 0, 0)
            load(1, 0, 1)
            over_chunks(sp, step)
            for par in range(2):
                sp.wait_ge(stored[par], NCH // 2 * 16)

        @block.gpsimd
        def _(pool):
            bias = keep["bias_o"][:].unsqueeze(1).to_broadcast([P, TPC, EMB])

            def add_bias(c, b, cc):
                par = cc % 2
                pool.wait_ge(data_in[par], uses(b, cc) * 32 + 32)
                if not (isinstance(b, int) and b == 0 and cc < 2):
                    pool.wait_ge(x2_done, (c - 1) * TPC)
                pool.tensor_tensor(xb[:, par], xin[:, par], bias, ALU.add).then_inc(biased, 1)

            def step(c, b, cc, more):
                pool.wait_ge(stats_done, c + 1)
                pool.tensor_tensor(var_eps[:], mean_var[:, :, 1], keep["eps"][:], ALU.add).then_inc(eps_added, 1)
                pool.wait_ge(eps_added, c + 1)
                pool.tensor_tensor(rstd[:], var_eps[:], keep["minus_half"][:], ALU.pow).then_inc(rstd_done, 1)
                last_two = isinstance(b, int) and cc >= CPB - 2
                if not last_two:
                    add_bias(c + 2, *after(b, cc, 2))

            add_bias(0, 0, 0)
            add_bias(1, 0, 1)
            over_chunks(pool, step)

        @block.vector
        def _(dve):
            def normalise(c, b, cc):
                par = cc % 2
                dve.wait_ge(biased, c + 1)
                if not (isinstance(b, int) and b == 0 and cc < 2):
                    dve.wait_ge(result_done, c - 1)
                for t in range(TPC):
                    dve.wait_ge(y_ready, c * TPC + 2 * (t // 2) + 2)
                    dve.tensor_tensor(x2[:, par, t], ps_y[:, t], xb[:, par, t], ALU.add).then_inc(x2_done, 1)
                    dve.wait_ge(x2_done, c * TPC + t + 1)
                    dve.bn_stats(stats[:, t], x2[:, par, t]).then_inc(stats_step, 1)
                dve.wait_ge(stats_step, c * TPC + TPC)
                carry(dve, passed)
                for t in range(TPC):
                    last = dve.bn_aggr(mean_var[:, t], stats[:, t])
                last.then_inc(stats_done, 1)
                dve.wait_ge(stats_done, c + 1)
                dve.wait_ge(rstd_done, c + 1)
                dve.wait_ge(turned, c * 2)
                for t in range(TPC):
                    last = dve.tensor_scalar(xn[:, t], x2[:, par, t], mean_var[:, t, 0:1], rstd[:, t:t + 1],
                                             ALU.subtract, ALU.mult)
                last.then_inc(xn_done, 1)

            def step(c, b, cc, more):
                if more:
                    normalise(c + 1, *after(b, cc, 1))
                dve.wait_ge(squash_done, c)
                for t in range(TPC):
                    dve.wait_ge(f_ready, c * TPC + 2 * (t // 2) + 2)
                    dve.tensor_tensor(pre[:, t], ps_f[:, t], keep["bias_f"][:], ALU.add).then_inc(pre_done, 1)
                dve.wait_ge(squash_done, c + 1)
                dve.wait_ge(stored[cc % 2], uses(b, cc) * 16)
                dve.tensor_tensor(result[:, cc % 2], x2[:, cc % 2], squashed[:], ALU.add).then_inc(result_done, 1)

            normalise(0, 0, 0)
            over_chunks(dve, step)

        @block.scalar
        def _(act):
            def step(c, b, cc, more):
                for half in range(HALVES):
                    act.wait_ge(turned, c * 2 + half + 1)
                    act.wait_ge(f_ready, c * TPC)
                    act.activation(xt[:, half], ps_turn[:, half], ACT.Copy).then_inc(turn_copied, 1)
                act.wait_ge(pre_done, c * TPC + TPC)
                act.wait_ge(result_done, c)
                act.activation(squashed[:], pre[:], ACT.Tanh).then_inc(squash_done, 1)

            over_chunks(act, step)

        @block.tensor
        def _(pe):
            def project_out(c, b, cc):
                par = cc % 2
                pe.wait_ge(data_in[par], uses(b, cc) * 32 + 32)
                for t in range(TPC):
                    if not (isinstance(c, int) and c == 0):
                        pe.wait_ge(x2_done, (c - 1) * TPC + 2 * (t // 2) + 2)
                    for k in range(HALVES):
                        last = pe.matmul(ps_y[:, t], ctx_in[:, par, k, t * P:(t + 1) * P], keep["w_o"][:, k],
                                         start=(k == 0), stop=(k == HALVES - 1))
                    last.then_inc(y_ready, 1)

            def step(c, b, cc, more):
                pe.wait_ge(xn_done, c + 1)
                for half in range(HALVES):
                    pe.wait_ge(turn_copied, c * 2)
                    carry(pe, passed)
                    for t in range(TPC):
                        last = pe.transpose(ps_turn[:, half, t * P:(t + 1) * P], xn[:, t, half * P:(half + 1) * P],
                                            ident[:])
                    last.then_inc(turned, 1)
                if more:
                    project_out(c + 1, *after(b, cc, 1))
                pe.wait_ge(turn_copied, c * 2 + 2)
                pe.wait_ge(pre_done, c * TPC)
                for t in range(TPC):
                    for k in range(HALVES):
                        last = pe.matmul(ps_f[:, t], xt[:, k, t * P:(t + 1) * P], keep["w_ffn"][:, k],
                                         start=(k == 0), stop=(k == HALVES - 1))
                    last.then_inc(f_ready, 1)

            project_out(0, 0, 0)
            over_chunks(pe, step)


def kernel(**inputs):
    import numpy as _np
    import concourse.bacc as _bacc
    from concourse import mybir as _mybir
    from concourse.bass_utils import run_bass_kernel_spmd as _run

    get = lambda name: _np.asarray(inputs["L0_" + name])
    bias = get("attn_in_proj_bias")
    arrays = {
        "x": get("attn_input_embeddings").reshape(BATCH * SEQ, EMB),
        "w_qkv_t": get("attn_in_proj_weight").T,
        "b_qk": bias[:2 * EMB].reshape(2 * HALVES, P).T,
        "b_v": bias[2 * EMB:],
        "w_o_t": get("attn_out_proj_weight").T,
        "b_o": get("attn_out_proj_bias"),
        "w1_t": get("ffn_weight").T,
        "a1_t": get("ffn_aux_weight1").T,
        "a2": get("ffn_aux_weight2"),
        "b_f": get("ffn_bias"),
    }
    nc = _bacc.Bacc("TRN2", target_bir_lowering=False, num_devices=1)
    feed, args = {}, []
    for name, a in arrays.items():
        a = _np.ascontiguousarray(a)
        feed["in_" + name] = a
        args.append(nc.dram_tensor("in_" + name, a.shape, _mybir.dt.from_np(a.dtype), kind="ExternalInput").ap())
    args.append(nc.dram_tensor("out_0", (BATCH * SEQ, EMB), F32, kind="ExternalOutput").ap())
    bass_preln_layer(nc, *args)
    r = _run(nc, [feed], core_ids=[0])
    return r.results[0]["out_0"].reshape(BATCH, SEQ, EMB)
```

```python
from contextlib import ExitStack

import concourse.bass as bass
from concourse import mybir

F32 = mybir.dt.float32
BF16 = mybir.dt.bfloat16
I32 = mybir.dt.int32
ALU = mybir.AluOpType
ACT = mybir.ActivationFunctionType
AX = mybir.AxisListType

P = 128
BATCH, SEQ, EMB, HEADS = 4, 2048, 256, 16
HD = EMB // HEADS
WINDOW = 16
EPS = 1e-5
CHUNK = 512
CPB = SEQ // CHUNK
NCH = BATCH * CPB
TPC = CHUNK // P
HALVES = EMB // P
KBS = SEQ // P
HG = 4
PAIRS = BATCH * HALVES
PARTS = 3
Q_ROWS = (0, 0, 1, 0, 2, 1)
K_ROWS = (0, 1, 0, 2, 0, 1)
DOT = len(Q_ROWS) * HD
CONTRACT = DOT + PARTS
BAND = P + WINDOW
LEAST_SUM = 1e-26
SUM_FLOOR = 1e-30
MARGIN = 1.02
NEG = -3.0e38


def carry(eng, passed):
    eng.sem_inc(passed, 1)


def bass_preln_layer(nc, x, w_qkv_t, b_qk, b_v, w_o_t, b_o, w1_t, a1_t, a2, b_f, out):
    q_parts = nc.dram_tensor("q_parts", (PAIRS, PARTS, P, SEQ), BF16, kind="Internal").ap()
    k_parts = nc.dram_tensor("k_parts", (PAIRS, PARTS, P, SEQ), BF16, kind="Internal").ap()
    guards = nc.dram_tensor("guards", (PAIRS, PARTS, HEADS // HALVES, SEQ), BF16, kind="Internal").ap()
    v_ones = nc.dram_tensor("v_ones", (PAIRS, 2, P, KBS, HG * 2 * HD), F32, kind="Internal").ap()
    context = nc.dram_tensor("context", (PAIRS, P, SEQ), F32, kind="Internal").ap()

    with ExitStack() as ctx:
        def sb(name, shape, dt=F32):
            return ctx.enter_context(nc.sbuf_tensor(name, shape, dt))

        keep = {
            "ident": sb("ident", [P, P]),
            "w_o": sb("w_o", [P, HALVES, EMB]),
            "w_ffn": sb("w_ffn", [P, HALVES, EMB]),
            "bias_o": sb("bias_o", [P, EMB]),
            "bias_f": sb("bias_f", [P, EMB]),
            "minus_half": sb("minus_half", [P, TPC]),
            "eps": sb("eps", [P, TPC]),
        }
        heads = {
            "qs": sb("qs", [CONTRACT, 2, HG, SEQ], BF16),
            "ks": sb("ks", [CONTRACT, 2, HG, SEQ], BF16),
            "vs": sb("vs", [P, 2, KBS, HG, 2 * HD]),
            "loaded": [ctx.enter_context(nc.semaphore(f"first_loaded{par}")) for par in range(2)],
        }
        project(nc, keep, heads, x, w_qkv_t, b_qk, b_v, w_o_t, b_o, w1_t, a1_t, a2, b_f,
                q_parts, k_parts, guards, v_ones)
        attend(nc, keep, heads, q_parts, k_parts, guards, v_ones, context)
        finish(nc, keep, x, context, out)


def load_heads(sp, heads, n, par, loaded, q_parts, k_parts, guards, v_ones, stages=range(3)):
    def src(parts_dram, part):
        return parts_dram[bass.ds(n, 1), part, par * 64:par * 64 + 64].rearrange("o (h d) t -> d (o h) t", h=HG)
    for r in range(len(Q_ROWS)):
        rows = slice(r * HD, (r + 1) * HD)
        if 0 in stages:
            sp.dma_start(heads["qs"][rows, par], src(q_parts, Q_ROWS[r])).then_inc(loaded, 16)
        if 1 in stages:
            sp.dma_start(heads["ks"][rows, par], src(k_parts, K_ROWS[r])).then_inc(loaded, 16)
    if 2 in stages:
        sp.dma_start(heads["qs"][DOT:CONTRACT, par], guards[bass.ds(n, 1), :, par * HG:(par + 1) * HG].rearrange(
            "o a h t -> (o a) h t")).then_inc(loaded, 16)
        sp.dma_start(heads["vs"][:, par].rearrange("p k h n -> p (k h n)"),
                     v_ones[bass.ds(n, 1), par].rearrange("o p k n -> (o p) (k n)")).then_inc(loaded, 16)


def project(nc, keep, heads, x, w_qkv_t, b_qk, b_v, w_o_t, b_o, w1_t, a1_t, a2, b_f,
            q_parts, k_parts, guards, v_ones):
    with ExitStack() as ctx:
        def sb(name, shape, dt=F32):
            return ctx.enter_context(nc.sbuf_tensor(name, shape, dt))

        def bank(name, shape):
            return ctx.enter_context(nc.psum_tensor(name, shape, F32))

        def sem(name):
            return ctx.enter_context(nc.semaphore(name))

        ident = keep["ident"]
        w_qkv = sb("w_qkv", [P, HALVES, 3 * EMB])
        bias_qk = sb("bias_qk", [P, 2 * HALVES])
        bias_v = sb("bias_v", [P, EMB])
        w1t = sb("w1t", [P, HALVES, EMB])
        a1t = sb("a1t", [P, HALVES, EMB])
        a2s = sb("a2s", [P, HALVES, EMB])
        a12 = sb("a12", [P, HALVES, EMB])
        head_of = sb("head_of", [P, HALVES, HEADS], BF16)
        xin = sb("xin", [P, 2, TPC, EMB])
        stats = sb("stats", [P, TPC, 6])
        mean_var = sb("mean_var", [P, TPC, 2])
        var_eps = sb("var_eps", [P, TPC])
        rstd = sb("rstd", [P, TPC])
        xn = sb("xn", [P, TPC, EMB])
        xt = sb("xt", [P, 2, HALVES, CHUNK])
        qk_f = sb("qk_f", [P, 4, CHUNK])
        rest = sb("rest", [P, 4, CHUNK])
        squares = sb("squares", [P, 4, CHUNK], BF16)
        parts = sb("parts", [P, 2, 4, PARTS, CHUNK], BF16)
        vaug = sb("vaug", [P, 2, HALVES * 2, TPC, HG, 2 * HD])
        q_sq = sb("q_sq", [HEADS, SEQ])
        k_sq = sb("k_sq", [HEADS, CPB])
        k_max = sb("k_max", [HEADS, 1])
        guard = sb("guard", [HEADS, PARTS, SEQ], BF16)

        ps_turn = [bank("ps_turn1", [P, CHUNK]), bank("ps_turn0", [P, CHUNK])]
        ps_norm = ps_turn[1]
        ps_qk = bank("ps_qk", [P, 4, CHUNK])
        ps_v = bank("ps_v", [P, TPC, EMB])

        passed = sem("passed")
        weights_in = sem("weights_in")
        consts = sem("consts")
        ones_set = sem("ones_set")
        a12_ready = sem("a12_ready")
        a12_copied = sem("a12_copied")
        x_in = [sem("x_in0"), sem("x_in1")]
        stats_step = sem("stats_step")
        stats_done = sem("stats_done")
        eps_added = sem("eps_added")
        rstd_done = sem("rstd_done")
        xn_done = sem("xn_done")
        turned = sem("turned")
        turn_copied = sem("turn_copied")
        qk_ready = sem("qk_ready")
        qk_copied = sem("qk_copied")
        squared = sem("squared")
        q_bias_scaled = sem("q_bias_scaled")
        rest_done = sem("rest_done")
        mid_done = sem("mid_done")
        low_done = sem("low_done")
        v_ready = sem("v_ready")
        v_copied = sem("v_copied")
        norms_ready = sem("norms_ready")
        norms_copied = sem("norms_copied")
        k_max_done = sem("k_max_done")
        bound_done = sem("bound_done")
        guard_done = sem("guard_done")
        parts_out = [sem("parts_out0"), sem("parts_out1")]
        v_out = [sem("v_out0"), sem("v_out1")]
        guard_out = sem("guard_out")

        WEIGHTS = 9
        x_tiles = x.rearrange("(c t p) e -> c p t e", t=TPC, p=P)
        block = ctx.enter_context(nc.Block())

        def over_chunks(eng, step):
            with eng.Fori(0, BATCH - 1) as b:
                for cc in range(CPB):
                    step(b * CPB + cc, b, cc, True)
            for cc in range(CPB):
                step((BATCH - 1) * CPB + cc, BATCH - 1, cc, cc < CPB - 1)

        def uses(b, cc):
            return b * (CPB // 2) + cc // 2

        @block.sync
        def _(sp):
            sp.dma_start(xin[:, 0], x_tiles[0]).then_inc(x_in[0], 16)
            sp.dma_start(xin[:, 1], x_tiles[1]).then_inc(x_in[1], 16)
            for dst, src in ((w_qkv, w_qkv_t), (keep["w_o"], w_o_t), (w1t, w1_t), (a1t, a1_t), (a2s, a2)):
                sp.dma_start(dst[:], src.rearrange("(h p) n -> p h n", p=P)).then_inc(weights_in, 16)
            sp.dma_start(bias_qk[:], b_qk).then_inc(weights_in, 16)
            for dst, src in ((bias_v, b_v), (keep["bias_o"], b_o), (keep["bias_f"], b_f)):
                sp.dma_start(dst[:], src.partition_broadcast(P)).then_inc(weights_in, 16)

            def store(c, b, cc, more):
                par = cc % 2
                last_two = isinstance(b, int) and cc >= CPB - 2
                if not last_two:
                    sp.wait_ge(xn_done, c + 1)
                    carry(sp, passed)
                    nxt = c + 2
                    src = x_tiles[nxt] if isinstance(nxt, int) else x_tiles[bass.ds(nxt, 1)].rearrange(
                        "o p t e -> (o p) t e")
                    sp.dma_start(xin[:, par], src).then_inc(x_in[par], 16)
                for j in range(4):
                    sp.wait_ge(low_done, c * 4 + j + 1 + 4)
                    carry(sp, passed)
                    dst = (q_parts, k_parts)[j // 2]
                    n = b * HALVES + j % 2
                    view = dst[bass.ds(n, 1), :, :, cc * CHUNK:(cc + 1) * CHUNK].rearrange("o a p t -> p (o a) t")
                    sp.dma_start(view, parts[:, par, j]).then_inc(parts_out[par], 16)
                sp.wait_ge(v_copied, c * TPC + TPC + TPC)
                carry(sp, passed)
                view = v_ones[bass.ds(b * HALVES, HALVES), :, :, cc * TPC:(cc + 1) * TPC].rearrange(
                    "f g p k n -> p (f g) (k n)")
                sp.dma_start(view, vaug[:, par].rearrange("p g k h n -> p g (k h n)")).then_inc(v_out[par], 16)
                if cc == CPB - 1:
                    sp.wait_ge(guard_done, b + 1)
                    carry(sp, passed)
                    for half in range(HALVES):
                        view = guards[bass.ds(b * HALVES + half, 1)].rearrange("o a h t -> h (o a) t")
                        sp.dma_start(view, guard[half * 8:half * 8 + 8]).then_inc(guard_out, 16)

            with sp.Fori(0, BATCH - 1) as b:
                for cc in range(CPB):
                    store(b * CPB + cc, b, cc, True)
            for cc in range(CPB):
                if cc == 0:
                    for par in range(2):
                        sp.wait_ge(parts_out[par], (CPB // 2) * 64)
                        sp.wait_ge(v_out[par], (CPB // 2) * 16)
                    sp.wait_ge(guard_out, 32)
                if cc < CPB - 1:
                    load_heads(sp, heads, 0, 0, heads["loaded"][0], q_parts, k_parts, guards, v_ones, stages=(cc,))
                store((BATCH - 1) * CPB + cc, BATCH - 1, cc, cc < CPB - 1)
            for par in range(2):
                sp.wait_ge(parts_out[par], NCH // 2 * 64)
                sp.wait_ge(v_out[par], NCH // 2 * 16)
            sp.wait_ge(guard_out, BATCH * 32)

        @block.gpsimd
        def _(pool):
            pool.memset(ident[:], 0.0).then_inc(consts, 1)
            pool.memset(head_of[:], 1.0).then_inc(consts, 1)
            pool.memset(keep["minus_half"][:], -0.5).then_inc(consts, 1)
            pool.memset(keep["eps"][:], EPS).then_inc(consts, 1)
            pool.memset(guard[:], 0.0).then_inc(consts, 1)
            pool.memset(vaug[:], 1.0).then_inc(consts, 1)
            pool.wait_ge(consts, 6)
            pool.affine_select(out=ident[:], in_=ident[:], compare_op=ALU.not_equal, fill=1.0, base=0,
                               pattern=[[-1, P]], channel_multiplier=1).then_inc(consts, 1)
            pool.affine_select(out=head_of[:], in_=head_of[:], compare_op=ALU.is_ge, fill=0.0, base=0,
                               pattern=[[P, HALVES], [-HD, HEADS]], channel_multiplier=1).then_inc(consts, 1)
            pool.wait_ge(consts, 8)
            pool.affine_select(out=head_of[:], in_=head_of[:], compare_op=ALU.is_ge, fill=0.0, base=HD - 1,
                               pattern=[[-P, HALVES], [HD, HEADS]], channel_multiplier=-1).then_inc(consts, 1)

            def rsqrt(c):
                pool.wait_ge(stats_done, c + 1)
                pool.tensor_tensor(var_eps[:], mean_var[:, :, 1], keep["eps"][:], ALU.add).then_inc(eps_added, 1)
                pool.wait_ge(eps_added, c + 1)
                pool.tensor_tensor(rstd[:], var_eps[:], keep["minus_half"][:], ALU.pow).then_inc(rstd_done, 1)

            for c in range(2 * HG):
                rsqrt(c)
                pool.wait_ge(rstd_done, c + 1)
                pool.memset(heads["ks"][DOT:CONTRACT, c // HG, c % HG], 1.0).then_inc(ones_set, 1)
                pool.wait_ge(ones_set, c + 1)
            with pool.Fori(2 * HG, NCH) as c:
                rsqrt(c)

        @block.vector
        def _(dve):
            dve.sem_inc(low_done, 4)
            dve.sem_inc(v_copied, TPC)

            def normalise_a(c, b, cc):
                par = cc % 2
                dve.wait_ge(x_in[par], uses(b, cc) * 16 + 16)
                for t in range(TPC):
                    dve.bn_stats(stats[:, t], xin[:, par, t]).then_inc(stats_step, 1)
                dve.wait_ge(stats_step, c * TPC + TPC)
                carry(dve, passed)
                for t in range(TPC):
                    last = dve.bn_aggr(mean_var[:, t], stats[:, t])
                last.then_inc(stats_done, 1)

            def normalise_b(c, b, cc):
                par = cc % 2
                dve.wait_ge(stats_done, c + 1)
                dve.wait_ge(rstd_done, c + 1)
                dve.wait_ge(turned, c * 2)
                for t in range(TPC):
                    last = dve.tensor_scalar(xn[:, t], xin[:, par, t], mean_var[:, t, 0:1], rstd[:, t:t + 1],
                                             ALU.subtract, ALU.mult)
                last.then_inc(xn_done, 1)

            def split(c, b, cc, j):
                par = cc % 2
                dve.wait_ge(qk_copied, c * 4 + j + 1)
                dve.tensor_tensor(rest[:, j], qk_f[:, j], parts[:, par, j, 0], ALU.subtract).then_inc(rest_done, 1)
                dve.wait_ge(rest_done, c * 4 + j + 1)
                dve.tensor_copy(parts[:, par, j, 1], rest[:, j]).then_inc(mid_done, 1)
                dve.wait_ge(mid_done, c * 4 + j + 1)
                dve.tensor_tensor(parts[:, par, j, 2], rest[:, j], parts[:, par, j, 1],
                                  ALU.subtract).then_inc(low_done, 1)

            def step(c, b, cc, more):
                par = cc % 2
                dve.wait_ge(parts_out[par], uses(b, cc) * 64)
                dve.wait_ge(v_out[par], uses(b, cc) * 16)
                nb, ncc = (b, cc + 1) if cc < CPB - 1 else (b + 1, 0)
                if more:
                    normalise_a(c + 1, nb, ncc)
                split(c, b, cc, 0)
                if more:
                    normalise_b(c + 1, nb, ncc)
                for j in range(1, 4):
                    split(c, b, cc, j)
                for t in range(TPC):
                    dve.wait_ge(v_ready, c * TPC + 2 * (t // 2) + 2)
                    dve.tensor_tensor(
                        vaug[:, par, :, t, :, 0:HD],
                        ps_v[:, t].rearrange("p (g h d) -> p g h d", g=HALVES * 2, h=HG),
                        bias_v[:].rearrange("p (g h d) -> p g h d", g=HALVES * 2, h=HG),
                        ALU.add).then_inc(v_copied, 1)
                dve.wait_ge(norms_ready, c + 1)
                if cc == 0:
                    dve.wait_ge(bound_done, b)
                dve.tensor_copy(q_sq[:, cc * CHUNK:(cc + 1) * CHUNK], ps_norm[0:HEADS]).then_inc(norms_copied, 1)
                dve.tensor_reduce(k_sq[:, cc:cc + 1], ps_norm[32:32 + HEADS], AX.X, ALU.max).then_inc(norms_copied, 1)
                if cc == CPB - 1:
                    dve.wait_ge(norms_copied, c * 2 + 2)
                    dve.tensor_reduce(k_max[:], k_sq[:], AX.X, ALU.max).then_inc(k_max_done, 1)
                    dve.wait_ge(bound_done, b + 1)
                    dve.wait_ge(guard_out, b * 32)
                    dve.tensor_scalar(guard[:, 0], q_sq[:], -MARGIN, None, ALU.mult).then_inc(guard_done, 1)

            normalise_a(0, 0, 0)
            dve.wait_ge(consts, 9)
            for half in range(HALVES):
                dve.wait_ge(a12_ready, HALVES)
                dve.tensor_copy(a12[:, half], ps_v[:, half]).then_inc(a12_copied, 1)
            for half in range(HALVES):
                dve.wait_ge(a12_ready, 2 * HALVES)
                dve.tensor_copy(keep["w_ffn"][:, half], ps_v[:, 2 + half]).then_inc(a12_copied, 1)
            normalise_b(0, 0, 0)
            over_chunks(dve, step)

        @block.scalar
        def _(act):
            act.sem_inc(squared, 4)
            act.wait_ge(weights_in, WEIGHTS * 16)
            act.activation(bias_qk[:, 0:HALVES], bias_qk[:, 0:HALVES], ACT.Copy, scale=HD ** -0.5).then_inc(q_bias_scaled, 1)
            act.wait_ge(q_bias_scaled, 1)

            def copy_turned(c, cc):
                for half in range(HALVES):
                    act.wait_ge(turned, c * 2 + half + 1)
                    act.activation(xt[:, cc % 2, half], ps_turn[half][:], ACT.Identity).then_inc(turn_copied, 1)

            def step(c, b, cc, more):
                par = cc % 2
                act.wait_ge(parts_out[par], uses(b, cc) * 64)
                for j in range(4):
                    scale = HD ** -0.5 if j < HALVES else 1.0
                    act.wait_ge(qk_ready, c * 4 + j + 1)
                    act.wait_ge(low_done, c * 4 + j + 1)
                    act.activation(qk_f[:, j], ps_qk[:, j], ACT.Identity, bias=bias_qk[:, j:j + 1], scale=scale)
                    act.activation(parts[:, par, j, 0], ps_qk[:, j], ACT.Identity, bias=bias_qk[:, j:j + 1],
                                   scale=scale).then_inc(qk_copied, 1)
                    act.wait_ge(norms_ready, c)
                    act.activation(squares[:, j], ps_qk[:, j], ACT.Square, bias=bias_qk[:, j:j + 1],
                                   scale=scale).then_inc(squared, 1)
                if more:
                    copy_turned(c + 1, cc + 1)
                if cc == CPB - 1:
                    act.wait_ge(k_max_done, b + 1)
                    act.wait_ge(guard_done, b)
                    act.activation(q_sq[:], q_sq[:], ACT.Sqrt, scale=k_max[:]).then_inc(bound_done, 1)

            copy_turned(0, 0)
            over_chunks(act, step)

        @block.tensor
        def _(pe):
            def turn(c, half):
                carry(pe, passed)
                for t in range(TPC):
                    last = pe.transpose(ps_turn[half][:, t * P:(t + 1) * P], xn[:, t, half * P:(half + 1) * P],
                                        ident[:])
                last.then_inc(turned, 1)

            pe.wait_ge(weights_in, WEIGHTS * 16)
            for stage, (left, right) in enumerate(((a1t, a2s), (w1t, a12))):
                if stage:
                    pe.wait_ge(a12_copied, HALVES)
                for half in range(HALVES):
                    for k in range(HALVES):
                        last = pe.matmul(ps_v[:, 2 * stage + half], left[:, k, half * P:(half + 1) * P], right[:, k],
                                         start=(k == 0), stop=(k == HALVES - 1))
                    last.then_inc(a12_ready, 1)
            pe.wait_ge(consts, 9)
            pe.wait_ge(xn_done, 1)
            turn(0, 0)
            turn(0, 1)
            pe.wait_ge(a12_copied, 2 * HALVES)

            def step(c, b, cc, more):
                par = cc % 2
                pe.wait_ge(turn_copied, c * 2 + 2)
                for j in range(4):
                    pe.wait_ge(squared, c * 4 + j + 1)
                    for k in range(HALVES):
                        last = pe.matmul(ps_qk[:, j], w_qkv[:, k, j * P:(j + 1) * P], xt[:, par, k],
                                         start=(k == 0), stop=(k == HALVES - 1))
                    last.then_inc(qk_ready, 1)
                if more:
                    pe.wait_ge(xn_done, c + 2)
                    turn(c + 1, 0)
                pe.wait_ge(norms_copied, c * 2)
                if more:
                    turn(c + 1, 1)
                for t in range(TPC):
                    pe.wait_ge(v_copied, c * TPC + 2 * (t // 2) + 2)
                    for k in range(HALVES):
                        last = pe.matmul(ps_v[:, t], xt[:, par, k, t * P:(t + 1) * P], w_qkv[:, k, 2 * EMB:],
                                         start=(k == 0), stop=(k == HALVES - 1))
                    last.then_inc(v_ready, 1)
                pe.wait_ge(squared, c * 4 + 4 + 4)
                if more:
                    pe.wait_ge(turn_copied, c * 2 + 4)
                for j in range(4):
                    at = 32 * (j // 2)
                    last = pe.matmul(ps_norm[at:at + HEADS], head_of[:, j % 2], squares[:, j],
                                     start=(j % 2 == 0), stop=(j % 2 == 1))
                last.then_inc(norms_ready, 1)

            over_chunks(pe, step)


def attend(nc, keep, heads, q_parts, k_parts, guards, v_ones, context):
    with ExitStack() as ctx:
        def sb(name, shape, dt=F32):
            return ctx.enter_context(nc.sbuf_tensor(name, shape, dt))

        def sem(name):
            return ctx.enter_context(nc.semaphore(name))

        RING = 32
        SBANKS = 6
        qs, ks, vs = heads["qs"], heads["ks"], heads["vs"]
        probs = sb("probs", [P, RING, CHUNK])
        allowed = sb("allowed", [P, BAND])
        blocked = sb("blocked", [P, BAND])
        blocked_bf = sb("blocked_bf", [P, BAND], BF16)
        ident_bf = sb("ident_bf", [P, P], BF16)
        sums = sb("sums", [P, CHUNK])
        inverse = sb("inverse", [P, CHUNK])
        ctx_t = sb("ctx_t", [P, 2, CHUNK])
        sums_fine = sb("sums_fine", [P, CHUNK])
        fine = sb("fine", [P, 1])
        bad = sb("bad", [P, 1])
        any_bad = sb("any_bad", [P, 1])
        flag = sb("flag", [1, 1], I32)
        row_max = sb("row_max", [P, HG * KBS])
        guard_f = sb("guard_f", [HG * KBS, P])
        guard_rest = sb("guard_rest", [HG * KBS, P])
        guard_parts = sb("guard_parts", [HG * KBS, PARTS, P], BF16)
        scores = ctx.enter_context(nc.psum_tensor("scores", [P, SBANKS, CHUNK], F32))
        outs = ctx.enter_context(nc.psum_tensor("outs", [P, 2, CHUNK], F32))

        passed = sem("a_passed")
        consts = sem("a_consts")
        fine_ready = sem("fine_ready")
        all_bad = sem("all_bad")
        flag_ready = sem("flag_ready")
        tile_ring = scores[:].rearrange("p b q -> p (b q)")
        prob_ring = probs[:].rearrange("p b q -> p (b q)")

        TILES = 2 * CPB * KBS * HG
        EXPS = TILES // 2
        UNITS = TILES // HG
        STEPS = 2 * CPB
        SPARE = RING // HG

        def masked_units():
            found = {}
            for s in range(STEPS):
                qc = s % CPB
                for kb in range(KBS):
                    at = kb * P - qc * CHUNK
                    lo, hi = max(at, 0), min(at + BAND, CHUNK)
                    if lo < hi:
                        found[s * KBS + kb] = (lo, hi - lo, lo - at)
            return found

        MASKED = masked_units()
        MASKS = 2 * len(MASKED)

        class Run:
            def __init__(self, tag, loaded=None):
                self.loaded = loaded or [sem(f"{tag}_loaded0"), sem(f"{tag}_loaded1")]
                self.scored = sem(f"{tag}_scored")
                self.exped = sem(f"{tag}_exped")
                self.masked = sem(f"{tag}_masked")
                self.summed = sem(f"{tag}_summed")
                self.out_free = sem(f"{tag}_out_free")
                self.shuffled = sem(f"{tag}_shuffled")
                self.inverted = sem(f"{tag}_inverted")
                self.checked = sem(f"{tag}_checked")
                self.stored = [sem(f"{tag}_stored0"), sem(f"{tag}_stored1")]

        EVACUATE_AT = {0: 5, 1: 9, 2: 3, 3: 4}

        def over_pairs(eng, body):
            with eng.Fori(0, PAIRS - 1) as n:
                body(n, True)
            body(PAIRS - 1, False)

        def bank_pair(e):
            return 1 if e == EXPS - 1 else e % (SBANKS // 2)

        def bank_user(e):
            before = max(x for x in range(-EXPS, e) if bank_pair(x % EXPS) == bank_pair(e))
            return before + 1

        first, again = Run("first", heads["loaded"]), Run("again")
        LOADS = 2 * len(Q_ROWS) + 2

        def load(sp, n, par, loaded, values=True):
            load_heads(sp, heads, n, par, loaded, q_parts, k_parts, guards, v_ones, range(3) if values else range(2))

        def run_sync(sp, r):
            if r is again:
                load(sp, 0, 0, r.loaded[0])
            load(sp, 0, 1, r.loaded[1])

            def body(n, more):
                for par in range(2):
                    for qc in range(CPB):
                        s = par * CPB + qc
                        sp.wait_ge(r.checked, n * STEPS + s + 1)
                        carry(sp, passed)
                        for g in range(HG):
                            at = par * 64 + g * HD
                            sp.dma_start(
                                context[bass.ds(n, 1), at:at + HD, qc * CHUNK:(qc + 1) * CHUNK].rearrange(
                                    "o d t -> (o d) t"),
                                ctx_t[32 * g:32 * g + HD, s % 2]).then_inc(r.stored[s % 2], 16)
                    if more:
                        sp.wait_ge(r.summed, n * UNITS + (par + 1) * UNITS // 2 + SPARE)
                        carry(sp, passed)
                        load(sp, n + 1, par, r.loaded[par])

            over_pairs(sp, body)
            for par in range(2):
                sp.wait_ge(r.stored[par], PAIRS * CPB * 64)

        def run_tensor(pe, r, block_first):
            def score(n, u):
                s, kb = divmod(u, KBS)
                par, qc = divmod(s, CPB)
                if kb == 0 and qc == 0:
                    pe.wait_ge(r.loaded[par], n * (LOADS * 16) + LOADS * 16)
                for h in range(HG):
                    e, side = divmod(u * HG + h, 2)
                    bank = 2 * bank_pair(e) + side
                    done = bank_user(e)
                    if side == 0 and not (done <= 0 and isinstance(n, int) and n == 0):
                        pe.wait_ge(r.exped, n * EXPS + done)
                    add = block_first and u in MASKED
                    last = pe.matmul(scores[:, bank], ks[:, par, h, kb * P:(kb + 1) * P],
                                     qs[:, par, h, qc * CHUNK:(qc + 1) * CHUNK], start=True, stop=not add)
                    if add:
                        lo, cols, at = MASKED[u]
                        last = pe.matmul(scores[:, bank, lo:lo + cols], ident_bf[:],
                                         blocked_bf[:, at:at + cols], start=False, stop=True)
                    if side == 1:
                        last.then_inc(r.scored, 1)

            def weigh(n, u):
                s, kb = divmod(u, KBS)
                par = s // CPB
                if kb == 0:
                    pe.wait_ge(r.out_free, n * STEPS + s + 1)
                pe.wait_ge(r.exped, n * EXPS + 2 * u + 2)
                if u in MASKED:
                    pe.wait_ge(r.masked, n * MASKS + 2 * (1 + sorted(MASKED).index(u)))
                for h in range(HG):
                    last = pe.matmul(outs[32 * h:32 * h + 32, s % 2], vs[:, par, kb, h],
                                     probs[:, (u * HG + h) % RING], start=(kb == 0), stop=(kb == KBS - 1))
                last.then_inc(r.summed, 1)

            def body(n, more):
                for u in range(UNITS):
                    if u + 2 < UNITS:
                        score(n, u + 2)
                    elif more:
                        score(n + 1, u + 2 - UNITS)
                    weigh(n, u)

            score(0, 0)
            score(0, 1)
            over_pairs(pe, body)

        def run_scalar(act, r):
            with act.Fori(0, PAIRS) as n:
                for e in range(EXPS):
                    act.wait_ge(r.scored, n * EXPS + e + 1)
                    act.wait_ge(r.summed, n * UNITS + (2 * e) // HG + 1)
                    a, b = 2 * bank_pair(e) * CHUNK, 2 * e % RING * CHUNK
                    act.activation(prob_ring[:, b:b + 2 * CHUNK], tile_ring[:, a:a + 2 * CHUNK],
                                   ACT.Exp).then_inc(r.exped, 1)

        def run_vector(dve, r):
            dve.sem_inc(r.summed, SPARE)
            dve.memset(sums_fine[:], 1.0).then_inc(r.out_free, 2)
            dve.wait_ge(r.out_free, 2)

            def evacuate(n, s):
                dve.wait_ge(r.summed, n * UNITS + (s + 1) * KBS + SPARE)
                dve.wait_ge(r.checked, n * STEPS + s)
                carry(dve, passed)
                dve.stream_shuffle(sums[:], outs[:, s % 2], mask=[HD] * 32).then_inc(r.shuffled, 1)
                dve.wait_ge(r.shuffled, n * STEPS + s + 1)
                dve.tensor_scalar(inverse[:], sums[:], SUM_FLOOR, None, ALU.max).then_inc(r.inverted, 1)
                dve.wait_ge(r.inverted, n * (2 * STEPS) + 2 * s + 1)
                dve.reciprocal(inverse[:], inverse[:]).then_inc(r.inverted, 1)
                dve.wait_ge(r.inverted, n * (2 * STEPS) + 2 * s + 2)
                dve.wait_ge(r.stored[s % 2], (n * (STEPS // 2) + s // 2) * 64)
                dve.tensor_tensor(ctx_t[:, s % 2], outs[:, s % 2], inverse[:], ALU.mult).then_inc(r.out_free, 1)
                dve.scalar_tensor_tensor(out=sums_fine[:], in0=sums[:], scalar=LEAST_SUM, in1=sums_fine[:],
                                         op0=ALU.is_ge, op1=ALU.mult).then_inc(r.checked, 1)

            def mask(n, u):
                lo, cols, at = MASKED[u]
                for e in (2 * u, 2 * u + 1):
                    dve.wait_ge(r.exped, n * EXPS + e + 1)
                    tiles = probs[:, 2 * e % RING:2 * e % RING + 2, lo:lo + cols]
                    keep_row = allowed[:, at:at + cols].unsqueeze(1).to_broadcast([P, 2, cols])
                    dve.tensor_tensor(tiles, tiles, keep_row, ALU.mult).then_inc(r.masked, 1)

            EARLY = EVACUATE_AT[0]

            def body(n, more):
                for u in range(EARLY, UNITS):
                    if u in MASKED:
                        mask(n, u)
                    s, kb = divmod(u, KBS)
                    if s and kb == EVACUATE_AT[s % CPB]:
                        evacuate(n, s - 1)
                for u in range(EARLY):
                    if more and u in MASKED:
                        mask(n + 1, u)
                evacuate(n, STEPS - 1)

            for u in range(EARLY):
                if u in MASKED:
                    mask(0, u)
            over_pairs(dve, body)

        g_loaded = sem("g_loaded")
        g_scored = sem("g_scored")
        g_blocked = sem("g_blocked")
        g_maxed = sem("g_maxed")
        g_turned = sem("g_turned")
        g_high = sem("g_high")
        g_step = sem("g_step")
        g_ready = sem("g_ready")
        g_stored = sem("g_stored")
        g_through = sem("g_through")
        ROWS = HG * KBS
        G_LOADS = 2 * len(Q_ROWS) * 16

        def groups(eng, body):
            with eng.Fori(0, PAIRS) as n:
                for par in range(2):
                    body(n, par, n * 2 + par)

        def maxima_sync(sp):
            def body(n, par, g):
                sp.wait_ge(g_maxed, g * ROWS)
                carry(sp, passed)
                load(sp, n, par, g_loaded, values=False)
                sp.wait_ge(g_ready, g + 1)
                carry(sp, passed)
                dst = guards[bass.ds(n, 1), :, par * HG:(par + 1) * HG].rearrange(
                    "o a h (k q) -> (o h k) a q", q=P)
                sp.dma_start(dst, guard_parts[:]).then_inc(g_stored, 16)
                sp.wait_ge(g_stored, g * 16 + 16)
                carry(sp, passed)
            groups(sp, body)

        def maxima_tensor(pe):
            def body(n, par, g):
                pe.wait_ge(g_loaded, g * G_LOADS + G_LOADS)
                for row in range(ROWS):
                    h, qb = divmod(row, KBS)
                    pe.wait_ge(g_maxed, g * ROWS + row)
                    for c in range(CPB):
                        last = pe.matmul(scores[:, c], qs[0:DOT, par, h, qb * P:(qb + 1) * P],
                                         ks[0:DOT, par, h, c * CHUNK:(c + 1) * CHUNK], start=True, stop=True)
                    last.then_inc(g_scored, 1)
                pe.wait_ge(g_maxed, g * ROWS + ROWS)
                carry(pe, passed)
                pe.transpose(outs[0:ROWS, 0, 0:P], row_max[:], keep["ident"][:]).then_inc(g_turned, 1)
            groups(pe, body)

        def maxima_vector(dve):
            def body(n, par, g):
                for row in range(ROWS):
                    qb = row % KBS
                    lo = max(qb * P - WINDOW, 0)
                    at = lo - (qb * P - WINDOW)
                    dve.wait_ge(g_scored, g * ROWS + row + 1)
                    band = tile_ring[:, lo:qb * P + P]
                    dve.tensor_tensor(band, band, blocked[:, at:BAND], ALU.add).then_inc(g_blocked, 1)
                    dve.wait_ge(g_blocked, g * ROWS + row + 1)
                    if row == 0:
                        dve.wait_ge(g_turned, g)
                    dve.tensor_reduce(row_max[:, row:row + 1], tile_ring[:, 0:SEQ], AX.X,
                                      ALU.max).then_inc(g_maxed, 1)
                dve.wait_ge(g_turned, g + 1)
                dve.wait_ge(g_stored, g * 16)
                dve.tensor_scalar(guard_f[:], outs[0:ROWS, 0, 0:P], -1.0, None, ALU.mult).then_inc(g_step, 1)
                dve.wait_ge(g_step, g * 4 + 1)
                dve.tensor_copy(guard_parts[:, 0], guard_f[:]).then_inc(g_step, 1)
                dve.wait_ge(g_step, g * 4 + 2)
                dve.tensor_tensor(guard_rest[:], guard_f[:], guard_parts[:, 0], ALU.subtract).then_inc(g_step, 1)
                dve.wait_ge(g_step, g * 4 + 3)
                dve.tensor_copy(guard_parts[:, 1], guard_rest[:]).then_inc(g_step, 1)
                dve.wait_ge(g_step, g * 4 + 4)
                dve.tensor_tensor(guard_parts[:, 2], guard_rest[:], guard_parts[:, 1],
                                  ALU.subtract).then_inc(g_ready, 1)
            groups(dve, body)

        block = ctx.enter_context(nc.Block())

        def if_bad(eng, body):
            eng.wait_ge(flag_ready, 1)
            found = eng.value_load(flag[0:1, 0:1], min_val=0, max_val=1)
            with eng.If(found > 0):
                body()

        @block.sync
        def _(sp):
            run_sync(sp, first)

            def general():
                maxima_sync(sp)
                run_sync(sp, again)
            if_bad(sp, general)

        @block.gpsimd
        def _(pool):
            pool.memset(allowed[:], 0.0).then_inc(consts, 1)
            pool.wait_ge(consts, 1)
            pool.affine_select(out=allowed[:], in_=allowed[:], compare_op=ALU.is_ge, fill=1.0, base=0,
                               pattern=[[1, BAND]], channel_multiplier=-1).then_inc(consts, 1)
            pool.wait_ge(consts, 2)
            pool.affine_select(out=allowed[:], in_=allowed[:], compare_op=ALU.is_ge, fill=1.0, base=WINDOW,
                               pattern=[[-1, BAND]], channel_multiplier=1).then_inc(consts, 1)
            pool.wait_ge(consts, 3)
            pool.tensor_scalar(blocked[:], allowed[:], 1.0, -NEG, ALU.subtract, ALU.mult).then_inc(consts, 1)
            pool.tensor_copy(ident_bf[:], keep["ident"][:]).then_inc(consts, 1)
            pool.wait_ge(consts, 5)
            pool.tensor_copy(blocked_bf[:], blocked[:]).then_inc(consts, 1)
            pool.wait_ge(fine_ready, 2)
            pool.partition_all_reduce(any_bad[:], bad[:], P, bass.bass_isa.ReduceOp.max).then_inc(all_bad, 1)

        @block.tensor
        def _(pe):
            run_tensor(pe, first, False)

            def general():
                pe.wait_ge(consts, 6)
                maxima_tensor(pe)
                pe.wait_ge(g_ready, 2 * PAIRS)
                run_tensor(pe, again, True)
            if_bad(pe, general)

        @block.scalar
        def _(act):
            run_scalar(act, first)
            if_bad(act, lambda: run_scalar(act, again))

        @block.vector
        def _(dve):
            dve.wait_ge(consts, 6)
            run_vector(dve, first)
            dve.wait_ge(first.checked, PAIRS * STEPS)
            dve.tensor_reduce(fine[:], sums_fine[:], AX.X, ALU.min).then_inc(fine_ready, 1)
            dve.wait_ge(fine_ready, 1)
            dve.tensor_scalar(bad[:], fine[:], -1.0, 1.0, ALU.mult, ALU.add).then_inc(fine_ready, 1)
            dve.wait_ge(all_bad, 1)
            dve.tensor_copy(flag[:], any_bad[0:1]).then_inc(flag_ready, 1)

            def general():
                maxima_vector(dve)
                run_vector(dve, again)
            if_bad(dve, general)


def finish(nc, keep, x, context, out):
    with ExitStack() as ctx:
        def sb(name, shape, dt=F32):
            return ctx.enter_context(nc.sbuf_tensor(name, shape, dt))

        def bank(name, shape):
            return ctx.enter_context(nc.psum_tensor(name, shape, F32))

        def sem(name):
            return ctx.enter_context(nc.semaphore(name))

        ident = keep["ident"]
        ctx_in = sb("ctx_in", [P, CPB, HALVES, CHUNK])
        xin = sb("f_xin", [P, CPB, TPC, EMB])
        x2 = sb("x2", [P, CPB, TPC, EMB])
        stats = sb("f_stats", [P, TPC, 6])
        mean_var = sb("f_mean_var", [P, TPC, 2])
        var_eps = sb("f_var_eps", [P, TPC])
        rstd = sb("f_rstd", [P, TPC])
        xn = sb("f_xn", [P, TPC, EMB])
        xt = sb("f_xt", [P, HALVES, CHUNK])
        pre = sb("pre", [P, TPC, EMB])
        squashed = sb("squashed", [P, TPC, EMB])
        result = sb("result", [P, 2, TPC, EMB])
        ps_y = bank("ps_y", [P, 2, TPC, EMB])
        ps_turn = bank("ps_turn", [P, HALVES, CHUNK])
        ps_f = bank("ps_f", [P, TPC, EMB])

        passed = sem("f_passed")
        data_in = [sem(f"data_in{cc}") for cc in range(CPB)]
        biased = sem("biased")
        y_ready = sem("y_ready")
        x2_done = sem("x2_done")
        stats_step = sem("f_stats_step")
        stats_done = sem("f_stats_done")
        eps_added = sem("f_eps_added")
        rstd_done = sem("f_rstd_done")
        xn_done = sem("f_xn_done")
        turned = sem("f_turned")
        turn_copied = sem("f_turn_copied")
        f_ready = sem("f_ready")
        pre_done = sem("pre_done")
        squash_done = sem("squash_done")
        result_done = sem("result_done")
        stored = [sem("f_stored0"), sem("f_stored1")]

        x_tiles = x.rearrange("(c t p) e -> c p t e", t=TPC, p=P)
        out_tiles = out.rearrange("(c t p) e -> c p t e", t=TPC, p=P)
        ctx_view = context.rearrange("(b f) p t -> b p f t", f=HALVES)
        block = ctx.enter_context(nc.Block())

        def over_chunks(eng, step):
            with eng.Fori(0, BATCH - 1) as b:
                for cc in range(CPB):
                    step(b * CPB + cc, b, cc)
            for cc in range(CPB):
                step((BATCH - 1) * CPB + cc, BATCH - 1, cc)

        def ahead(b, cc, k):
            nb, ncc = b + (cc + k) // CPB, (cc + k) % CPB
            if isinstance(b, int) and nb >= BATCH:
                return None
            return nb * CPB + ncc, nb, ncc

        @block.sync
        def _(sp):
            def load(c, b, cc):
                sp.dma_start(ctx_in[:, cc], ctx_view[bass.ds(b, 1), :, :, cc * CHUNK:(cc + 1) * CHUNK].rearrange(
                    "o p f t -> (o p) f t")).then_inc(data_in[cc], 16)
                sp.dma_start(xin[:, cc], x_tiles[bass.ds(c, 1)].rearrange("o p t e -> (o p) t e")
                             ).then_inc(data_in[cc], 16)

            def step(c, b, cc):
                nxt = ahead(b, cc, CPB)
                if nxt:
                    sp.wait_ge(y_ready, c * TPC + TPC)
                    carry(sp, passed)
                    sp.wait_ge(biased, c + 1)
                    carry(sp, passed)
                    load(*nxt)
                sp.wait_ge(result_done, c + 1)
                carry(sp, passed)
                sp.dma_start(out_tiles[bass.ds(c, 1)].rearrange("o p t e -> (o p) t e"),
                             result[:, cc % 2]).then_inc(stored[cc % 2], 16)

            for cc in range(CPB):
                load(cc, 0, cc)
            over_chunks(sp, step)
            for par in range(2):
                sp.wait_ge(stored[par], NCH // 2 * 16)

        @block.gpsimd
        def _(pool):
            bias = keep["bias_o"][:].unsqueeze(1).to_broadcast([P, TPC, EMB])

            def add_bias(c, b, cc):
                pool.wait_ge(data_in[cc], b * 32 + 32)
                pool.tensor_tensor(x2[:, cc], xin[:, cc], bias, ALU.add).then_inc(biased, 1)

            def rsqrt(c, b, cc):
                pool.wait_ge(stats_done, c + 1)
                pool.tensor_tensor(var_eps[:], mean_var[:, :, 1], keep["eps"][:], ALU.add).then_inc(eps_added, 1)
                pool.wait_ge(eps_added, c + 1)
                pool.tensor_tensor(rstd[:], var_eps[:], keep["minus_half"][:], ALU.pow).then_inc(rstd_done, 1)

            def step(c, b, cc):
                if ahead(b, cc, 3):
                    pool.wait_ge(result_done, c)
                    add_bias(*ahead(b, cc, 3))
                if ahead(b, cc, 2):
                    rsqrt(*ahead(b, cc, 2))

            add_bias(0, 0, 0)
            rsqrt(0, 0, 0)
            add_bias(1, 0, 1)
            rsqrt(1, 0, 1)
            add_bias(2, 0, 2)
            over_chunks(pool, step)

        @block.vector
        def _(dve):
            def add_attention(c, b, cc):
                dve.wait_ge(biased, c + 1)
                for t in range(TPC):
                    dve.wait_ge(y_ready, c * TPC + 2 * (t // 2) + 2)
                    dve.tensor_tensor(x2[:, cc, t], ps_y[:, cc % 2, t], x2[:, cc, t], ALU.add).then_inc(x2_done, 1)
                for t in range(TPC):
                    dve.wait_ge(x2_done, c * TPC + t + 1)
                    dve.bn_stats(stats[:, t], x2[:, cc, t]).then_inc(stats_step, 1)
                dve.wait_ge(stats_step, c * TPC + TPC)
                carry(dve, passed)
                for t in range(TPC):
                    last = dve.bn_aggr(mean_var[:, t], stats[:, t])
                last.then_inc(stats_done, 1)

            def normalise(c, b, cc):
                dve.wait_ge(stats_done, c + 1)
                dve.wait_ge(rstd_done, c + 1)
                dve.wait_ge(turned, c * 2)
                for t in range(TPC):
                    last = dve.tensor_scalar(xn[:, t], x2[:, cc, t], mean_var[:, t, 0:1], rstd[:, t:t + 1],
                                             ALU.subtract, ALU.mult)
                last.then_inc(xn_done, 1)

            def step(c, b, cc):
                if ahead(b, cc, 1):
                    normalise(*ahead(b, cc, 1))
                if ahead(b, cc, 2):
                    add_attention(*ahead(b, cc, 2))
                dve.wait_ge(squash_done, c)
                for t in range(TPC):
                    dve.wait_ge(f_ready, c * TPC + 2 * (t // 2) + 2)
                    dve.tensor_tensor(pre[:, t], ps_f[:, t], keep["bias_f"][:], ALU.add).then_inc(pre_done, 1)
                dve.wait_ge(squash_done, c + 1)
                dve.wait_ge(stored[cc % 2], b * 32 + cc // 2 * 16)
                dve.tensor_tensor(result[:, cc % 2], x2[:, cc], squashed[:], ALU.add).then_inc(result_done, 1)

            add_attention(0, 0, 0)
            normalise(0, 0, 0)
            add_attention(1, 0, 1)
            over_chunks(dve, step)

        @block.scalar
        def _(act):
            def step(c, b, cc):
                for half in range(HALVES):
                    act.wait_ge(turned, c * 2 + half + 1)
                    act.wait_ge(f_ready, c * TPC)
                    act.activation(xt[:, half], ps_turn[:, half], ACT.Copy).then_inc(turn_copied, 1)
                act.wait_ge(pre_done, c * TPC + TPC)
                act.wait_ge(result_done, c)
                act.activation(squashed[:], pre[:], ACT.Tanh).then_inc(squash_done, 1)

            over_chunks(act, step)

        @block.tensor
        def _(pe):
            def project_out(c, b, cc):
                pe.wait_ge(data_in[cc], b * 32 + 32)
                for t in range(TPC):
                    if not (isinstance(b, int) and b == 0 and cc < 2):
                        pe.wait_ge(x2_done, (c - 2) * TPC + 2 * (t // 2) + 2)
                    for k in range(HALVES):
                        last = pe.matmul(ps_y[:, cc % 2, t], ctx_in[:, cc, k, t * P:(t + 1) * P], keep["w_o"][:, k],
                                         start=(k == 0), stop=(k == HALVES - 1))
                    last.then_inc(y_ready, 1)

            def step(c, b, cc):
                pe.wait_ge(xn_done, c + 1)
                pe.wait_ge(turn_copied, c * 2)
                carry(pe, passed)
                for half in range(HALVES):
                    for t in range(TPC):
                        last = pe.transpose(ps_turn[:, half, t * P:(t + 1) * P], xn[:, t, half * P:(half + 1) * P],
                                            ident[:])
                    last.then_inc(turned, 1)
                if ahead(b, cc, 2):
                    project_out(*ahead(b, cc, 2))
                pe.wait_ge(turn_copied, c * 2 + 2)
                pe.wait_ge(pre_done, c * TPC)
                for t in range(TPC):
                    for k in range(HALVES):
                        last = pe.matmul(ps_f[:, t], xt[:, k, t * P:(t + 1) * P], keep["w_ffn"][:, k],
                                         start=(k == 0), stop=(k == HALVES - 1))
                    last.then_inc(f_ready, 1)

            project_out(0, 0, 0)
            project_out(1, 0, 1)
            over_chunks(pe, step)


def kernel(**inputs):
    import numpy as _np
    import concourse.bacc as _bacc
    from concourse import mybir as _mybir
    from concourse.bass_utils import run_bass_kernel_spmd as _run

    get = lambda name: _np.asarray(inputs["L0_" + name])
    bias = get("attn_in_proj_bias")
    arrays = {
        "x": get("attn_input_embeddings").reshape(BATCH * SEQ, EMB),
        "w_qkv_t": get("attn_in_proj_weight").T,
        "b_qk": bias[:2 * EMB].reshape(2 * HALVES, P).T,
        "b_v": bias[2 * EMB:],
        "w_o_t": get("attn_out_proj_weight").T,
        "b_o": get("attn_out_proj_bias"),
        "w1_t": get("ffn_weight").T,
        "a1_t": get("ffn_aux_weight1").T,
        "a2": get("ffn_aux_weight2"),
        "b_f": get("ffn_bias"),
    }
    nc = _bacc.Bacc("TRN2", target_bir_lowering=False, num_devices=1)
    feed, args = {}, []
    for name, a in arrays.items():
        a = _np.ascontiguousarray(a)
        feed["in_" + name] = a
        args.append(nc.dram_tensor("in_" + name, a.shape, _mybir.dt.from_np(a.dtype), kind="ExternalInput").ap())
    args.append(nc.dram_tensor("out_0", (BATCH * SEQ, EMB), F32, kind="ExternalOutput").ap())
    bass_preln_layer(nc, *args)
    r = _run(nc, [feed], core_ids=[0])
    return r.results[0]["out_0"].reshape(BATCH, SEQ, EMB)
```
